# Optimizing a Trainium2 kernel written in Bass

```python
import numpy as np
import jax
import jax.numpy as jnp

def _softmax(x, axis=-1):
    return jax.nn.softmax(x, axis=axis)

def _gelu(x):
    return jax.nn.gelu(x, approximate=True)

def _silu(x):
    return jax.nn.silu(x)

def _sigmoid(x):
    return jax.nn.sigmoid(x)

def _layernorm(x, axis=-1, eps=1e-05):
    m = jnp.mean(x, axis=axis, keepdims=True)
    v = jnp.var(x, axis=axis, keepdims=True)
    return (x - m) / jnp.sqrt(v + eps)

def _scatter_add(tgt, idx, src, axis=0):
    return tgt.at[idx].add(src)

def _segment_sum(src, seg, n):
    return jax.ops.segment_sum(src, seg, n)
kernel_name = 'mk_gnn_preln_d1_gnn_r32_3cd037'

def setup_inputs(seed: int=0):
    np.random.seed(seed)
    _w = jnp.asarray

    def _rec_inputs():
        import jax
        import jax.numpy as jnp
        _gk = jax.random.key(seed)
        x = -0.0003713 + 1 * jax.random.normal(jax.random.fold_in(_gk, 1), (3125, 256), jnp.float32)
        _s = jax.random.randint(jax.random.fold_in(_gk, 2), (25000,), 0, 3125, jnp.int32)
        _d = jax.random.randint(jax.random.fold_in(_gk, 3), (25000,), 0, 3125, jnp.int32)
        _loop = jnp.arange(3125, dtype=jnp.int32)
        src = jnp.concatenate([_s, _d, _loop])
        dst = jnp.concatenate([_d, _s, _loop])
        _o = jnp.argsort(dst, stable=True)
        src = src[_o]
        dst = dst[_o]
        edge_attr_4 = jax.random.uniform(jax.random.fold_in(_gk, 11), (53125, 4), jnp.float32, 0.0, 0.999999)
        return (x, src, dst, edge_attr_4)
    x, src, dst, edge_attr_4 = _rec_inputs()

    def _L0_gnn_setup():
        import jax, jax.numpy as jnp
        import numpy as np
        N_NODES = 50000
        N_EDGES = 10000
        HIDDEN = 256
        N_LAYERS = 5
        BN_EPS = 1e-05

        def _mpnn(x, edge_index, edge_attr, mlp_w, mlp_b, ew1, ew2, bn_g, bn_b):
            n = x.shape[0]
            row, col = (edge_index[0], edge_index[1])
            deg = jax.ops.segment_sum(jnp.ones((edge_index.shape[1],), x.dtype), col, num_segments=n)
            dinv = jnp.where(deg > 0, deg ** (-0.5), 0.0)
            norm = dinv[row] * dinv[col]
            h = x
            for l in range(N_LAYERS):
                edge_fea = jnp.concatenate([edge_attr[:, 3:] @ ew1[l], edge_attr[:, 0:3] @ ew2[l]], axis=-1)
                msg = norm[:, None] * (h[row] + edge_fea)
                agg = jax.ops.segment_sum(msg, col, num_segments=n)
                h = jax.nn.relu(jnp.concatenate([h, agg], axis=1) @ mlp_w[l] + mlp_b[l])
                mu = h.mean(axis=0)
                var = h.var(axis=0)
                h = (h - mu) * jax.lax.rsqrt(var + BN_EPS) * bn_g[l] + bn_b[l]
                if l != N_LAYERS - 1:
                    h = jax.nn.relu(h)
            return h
        key = jax.random.key(seed)
        ks = jax.random.split(key, 8)
        x = jax.random.normal(ks[0], (N_NODES, HIDDEN), dtype=jnp.float32)
        edge_index = jax.random.randint(ks[1], (2, N_EDGES), 0, N_NODES, dtype=jnp.int64)
        edge_attr = jax.random.uniform(ks[2], (N_EDGES, 4), dtype=jnp.float32)
        mlp_w = jax.random.normal(ks[3], (N_LAYERS, 2 * HIDDEN, HIDDEN), dtype=jnp.float32) * (1.0 / np.sqrt(2 * HIDDEN))
        mlp_b = jnp.zeros((N_LAYERS, HIDDEN), dtype=jnp.float32)
        ew1 = jax.random.normal(ks[4], (N_LAYERS, 1, HIDDEN // 2), dtype=jnp.float32)
        ew2 = jax.random.normal(ks[5], (N_LAYERS, 3, HIDDEN // 2), dtype=jnp.float32) * (1.0 / np.sqrt(3.0))
        bn_g = jnp.ones((N_LAYERS, HIDDEN), dtype=jnp.float32)
        bn_b = jnp.zeros((N_LAYERS, HIDDEN), dtype=jnp.float32)
        return {'x': x, 'edge_index': edge_index, 'edge_attr': edge_attr, 'mlp_w': mlp_w, 'mlp_b': mlp_b, 'ew1': ew1, 'ew2': ew2, 'bn_g': bn_g, 'bn_b': bn_b}
    _L0_gnn_all = _L0_gnn_setup()
    _L0_gnn_in = {k: v for k, v in _L0_gnn_all.items() if k in ('mlp_w', 'mlp_b', 'ew1', 'ew2', 'bn_g', 'bn_b')}
    del _L0_gnn_all
    return {'x': x, 'src': src, 'dst': dst, 'edge_attr_4': edge_attr_4, 'L0_gnn_mlp_w': _L0_gnn_in['mlp_w'], 'L0_gnn_mlp_b': _L0_gnn_in['mlp_b'], 'L0_gnn_ew1': _L0_gnn_in['ew1'], 'L0_gnn_ew2': _L0_gnn_in['ew2'], 'L0_gnn_bn_g': _L0_gnn_in['bn_g'], 'L0_gnn_bn_b': _L0_gnn_in['bn_b']}

def reference(x, src, dst, edge_attr_4, L0_gnn_mlp_w, L0_gnn_mlp_b, L0_gnn_ew1, L0_gnn_ew2, L0_gnn_bn_g, L0_gnn_bn_b):
    import jax
    import jax.numpy as jnp

    def _L0_gnn_ref(x, edge_index, edge_attr, mlp_w, mlp_b, ew1, ew2, bn_g, bn_b):
        import jax, jax.numpy as jnp
        import numpy as np
        N_NODES = 50000
        N_EDGES = 10000
        HIDDEN = 256
        N_LAYERS = 5
        BN_EPS = 1e-05

        def _mpnn(x, edge_index, edge_attr, mlp_w, mlp_b, ew1, ew2, bn_g, bn_b):
            n = x.shape[0]
            row, col = (edge_index[0], edge_index[1])
            deg = jax.ops.segment_sum(jnp.ones((edge_index.shape[1],), x.dtype), col, num_segments=n)
            dinv = jnp.where(deg > 0, deg ** (-0.5), 0.0)
            norm = dinv[row] * dinv[col]
            h = x
            for l in range(N_LAYERS):
                edge_fea = jnp.concatenate([edge_attr[:, 3:] @ ew1[l], edge_attr[:, 0:3] @ ew2[l]], axis=-1)
                msg = norm[:, None] * (h[row] + edge_fea)
                agg = jax.ops.segment_sum(msg, col, num_segments=n)
                h = jax.nn.relu(jnp.concatenate([h, agg], axis=1) @ mlp_w[l] + mlp_b[l])
                mu = h.mean(axis=0)
                var = h.var(axis=0)
                h = (h - mu) * jax.lax.rsqrt(var + BN_EPS) * bn_g[l] + bn_b[l]
                if l != N_LAYERS - 1:
                    h = jax.nn.relu(h)
            return h
        return _mpnn(x, edge_index, edge_attr, mlp_w, mlp_b, ew1, ew2, bn_g, bn_b)
    edge_index = jnp.stack([src, dst])
    h = jnp.maximum(_layernorm(x, axis=-1), 0.0)
    x = x + _L0_gnn_ref(h, edge_index, edge_attr_4, L0_gnn_mlp_w, L0_gnn_mlp_b, L0_gnn_ew1, L0_gnn_ew2, L0_gnn_bn_g, L0_gnn_bn_b)
    return x

_drawn_inputs = setup_inputs


def setup_inputs(seed=0):
    import zlib

    import numpy as np

    out = dict(_drawn_inputs(seed))
    spreads = {'L0_gnn_mlp_b': (0.0, 0.1), 'L0_gnn_bn_g': (1.0, 0.2), 'L0_gnn_bn_b': (0.0, 0.1)}
    factors = {}
    for name, (base, spread) in spreads.items():
        noise = np.random.default_rng([zlib.crc32(name.encode()), seed]).standard_normal(out[name].shape)
        drawn = base * np.exp(spread * noise) if base else spread * noise
        out[name] = jnp.asarray(drawn.astype(out[name].dtype))
    for name, factor in factors.items():
        out[name] = (out[name] * factor).astype(out[name].dtype)
    return out
```

```python
import concourse.bass as bass
from concourse import mybir
from contextlib import ExitStack


def gnn_program(nc, x, src, dst, edge_attr, mlp_w, mlp_b, ew1, ew2, bn_g, bn_b, out):
    f32, f16, i32 = mybir.dt.float32, mybir.dt.float16, mybir.dt.int32
    ALU, ACT, AX = mybir.AluOpType, mybir.ActivationFunctionType, mybir.AxisListType

    P = 128
    N, D = x.shape
    E = src.shape[0]
    K_ATTR = edge_attr.shape[1]
    L = mlp_w.shape[0]
    HALVES = D // P
    BLOCKS = -(-N // P)
    TAIL = N - (BLOCKS - 1) * P
    LO, HI = 64, 49
    NP = LO * HI
    WIN = 16
    NW = NP // WIN
    WQ = LO // WIN
    WKEYS = BLOCKS * WIN
    WT = 3
    CAP = WT * P
    UN = 4
    CH = 448
    NCH = NP // CH
    LAST_CH = N - (NCH - 1) * CH
    EPP = 420
    EP = P * EPP
    ROWS = E // EPP
    REST = E - ROWS * EPP
    PAD_DST = 4000
    GRP = 2
    HALF = EP // GRP
    LC = 480
    LSTEPS = HALF // LC
    HCH = 70
    HSTEPS = EPP // HCH
    TW = 8
    DSCALE = 1024.0
    HSCALE = 256.0
    EPS = 1e-5
    BQ = 5
    NBQ = BLOCKS // BQ
    assert NP >= N and NP % CH == 0 and EP >= E + CAP and BLOCKS * P >= N and D == 2 * P
    assert HALF % LC == 0 and LSTEPS % 8 == 0 and EPP % HCH == 0 and HSTEPS % 2 == 0 and NW % UN == 0
    assert BLOCKS % BQ == 0 and TAIL <= LO

    ctx = ExitStack()
    with ctx:
        ctx.enter_context(nc.allow_non_contiguous_dma(reason="short tables, once"))

        def sb(name, shape, dt):
            return ctx.enter_context(nc.sbuf_tensor(name, shape, dt))

        def sem(name):
            return ctx.enter_context(nc.semaphore(name))

        edge_table = nc.dram_tensor("edge_table", [EP, TW], f32).ap()
        src_lo_dram = nc.dram_tensor("src_lo_dram", [EP], f16).ap()
        src_hi_dram = nc.dram_tensor("src_hi_dram", [EP], f16).ap()
        src_factor_dram = nc.dram_tensor("src_factor_dram", [EP], f32).ap()
        dst_factor_dram = nc.dram_tensor("dst_factor_dram", [NP], f32).ap()
        starts_dram = nc.dram_tensor("starts_dram", [NW], i32).ap()

        countsT = sb("countsT", [P, BLOCKS * NP], f16)
        hT = sb("hT", [P, HALVES * NP], f32)
        hs = sb("hs", [P, BLOCKS * 2 * D], f16)
        work = sb("work", [P, 2816], f32)
        hT3 = hT[:, :].rearrange("p (f n) -> p f n", f=HALVES)
        hs4 = hs[:, :].rearrange("p (i s f) -> p i s f", i=BLOCKS, s=2)
        counts3 = countsT[:, :].rearrange("p (a n) -> p a n", a=BLOCKS)

        iota_row = sb("iota_row", [P, CH], f16)
        zeros16 = sb("zeros16", [P, CH], f16)
        ident = sb("ident", [P, P], f32)
        win_node = sb("win_node", [P, NW], f32)
        win_key = sb("win_key", [P, NW], f32)
        starts_row = sb("starts_row", [1, NW], i32)
        flag_row = sb("flag_row", [1, 1], i32)
        edge_buf = sb("edge_buf", [P, UN, WT, TW], f32)
        dcol = sb("dcol", [P, BLOCKS], f32)
        ewt = sb("ewt", [P, D], f32)
        aff = sb("aff", [P, 3, L * HALVES], f32)
        stats = sb("stats", [P, HALVES * NCH * 6], f32)
        small = sb("small", [P, 24], f32)
        mv = sb("mv", [P, 4 * BLOCKS], f32)
        mv_a = sb("mv_a", [P, 2 * BLOCKS], f32)

        def early(lo, n, dt=f16):
            view = countsT[:, lo:lo + n]
            return view if dt == f16 else view.bitcast(dt)
        lo_bc = early(0, HALF)
        hi_bc = early(HALF, HALF)
        at = GRP * HALF
        oh_lo = early(at, 2 * HCH * LO).rearrange("p (b t v) -> p b t v", b=2, v=LO)
        oh_hi = early(at + 2 * HCH * LO, 2 * HCH * HI).rearrange("p (b t v) -> p b t v", b=2, v=HI)
        factor_rows = early(at, 2 * 2 * 4 * LC, f32).rearrange("p (b n) -> p b n", b=2)
        picked = early(at + 16 * LC, 2 * 2 * LC, f32).rearrange("p (b n) -> p b n", b=2)
        table_at = at + 2 * HCH * (LO + HI)
        table_tile = early(table_at, 2 * EPP * TW, f32).rearrange("p (e w) -> p e w", w=TW)
        assert 20 * LC <= 2 * HCH * (LO + HI) and table_at + 2 * EPP * TW <= BLOCKS * NP

        hs_f = hs[:, :].bitcast(f32)
        src_f = hs_f[:, 0:EPP]
        dst_f = hs_f[:, EPP:2 * EPP]
        src_i = hs_f[:, 2 * EPP:3 * EPP].bitcast(i32)
        dst_i = hs_f[:, 3 * EPP:4 * EPP].bitcast(i32)
        tmp_i = hs_f[:, 4 * EPP:5 * EPP].bitcast(i32)
        next_i = hs_f[:, 5 * EPP:6 * EPP].bitcast(i32)
        attr16 = hs_f[:, 6 * EPP:10 * EPP].bitcast(f16).rearrange("p (e k) -> p e k", k=2 * K_ATTR)
        all_dst = hs_f[:, 10 * EPP:10 * EPP + NP // 2].bitcast(f16)
        all_src = hs_f[:, 10 * EPP + NP // 2:10 * EPP + NP // 2 + P // 2].bitcast(f16)
        x_tiles = hs_f[:, 0:BLOCKS * D].rearrange("p (i f) -> p i f", i=BLOCKS)

        attr = hT[:, 0:EPP * K_ATTR].rearrange("p (e k) -> p e k", k=K_ATTR)
        q = EPP * K_ATTR
        src_factor = hT[:, q:q + EPP]
        src_lo = hT[:, q + EPP:q + EPP + EPP // 2].bitcast(f16)
        src_hi = hT[:, q + EPP + EPP // 2:q + 2 * EPP].bitcast(f16)
        dst_lo = hT[:, q + 2 * EPP:q + 2 * EPP + EPP // 2].bitcast(f16)
        dst_hi = hT[:, q + 2 * EPP + EPP // 2:q + 3 * EPP].bitcast(f16)
        disorder = hT[:, q + 3 * EPP:q + 4 * EPP]
        q2 = q + 4 * EPP
        deg = hT[:, q2:q2 + HI]
        dinv = hT[:, q2 + 64:q2 + 64 + HI]
        t1 = hT[:, q2 + 128:q2 + 128 + HI]
        t2 = hT[:, q2 + 192:q2 + 192 + HI]
        t3 = hT[:, q2 + 256:q2 + 256 + HI]
        ones_t = hT[:, q2 + 320:q2 + 320 + HI]
        twice = hT[:, q2 + 384:q2 + 384 + P]
        group_of = hT[:, q2 + 512:q2 + 514]
        lanes = hT[:, q2 + 514:q2 + 515]
        lane_lo = hT[:, q2 + 515:q2 + 516]
        lane_hi = hT[:, q2 + 516:q2 + 517]
        steps5 = hT[:, q2 + 520:q2 + 525]
        below = hT[:, q2 + 530:q2 + 535]
        within = hT[:, q2 + 540:q2 + 544]
        bad = hT[:, q2 + 545:q2 + 546]
        bad4 = hT[:, q2 + 546:q2 + 547]
        ones1 = hT[:, q2 + 547:q2 + 548]
        starts_i = hT[:, q2 + 550:q2 + 550 + HI].bitcast(i32)
        dblk = hT[:, q2 + 600:q2 + 600 + P].bitcast(f16).rearrange("p (s c) -> p s c", s=2)
        assert q2 + 600 + P <= HALVES * NP
        attr_sums = hT[0:K_ATTR, 0:NP]
        attr_parts = hT[0:K_ATTR, NP:2 * NP].bitcast(f16).rearrange("p (s n) -> p s n", s=2)

        work16 = work[:, :].bitcast(f16)
        oh_key = work16[:, 0:2 * WT * WKEYS].rearrange("p (b k v) -> p b k v", b=2, k=WT)
        o = 2 * WT * WKEYS
        oh_src = work16[:, o:o + 2 * WT * P].rearrange("p (b k v) -> p b k v", b=2, k=WT)
        o += 2 * WT * P
        oh_dst = work16[:, o:o + 2 * WT * WIN].rearrange("p (b k v) -> p b k v", b=2, k=WT)
        weights = work[:, 0:4 * D].rearrange("p (k n) -> p k n", k=4)
        agg = work[:, 4 * D:4 * D + 2 * CH].rearrange("p (f n) -> p f n", f=HALVES)
        dst_factor = work[:, 4 * D + 2 * CH:4 * D + 3 * CH]

        banks = [ctx.enter_context(nc.psum_tensor(f"bank{n}", [P, 512], f32)) for n in range(8)]

        s_pads, s_src, s_dst, s_next, s_attr = (sem(n) for n in ("s_pads", "s_src", "s_dst", "s_next", "s_attr"))
        s_iota, s_ident0, s_ident = sem("s_iota"), sem("s_ident0"), sem("s_ident")
        s_dve1, s_codes, s_codes_out, s_bc = sem("s_dve1"), sem("s_codes"), sem("s_codes_out"), sem("s_bc")
        s_hist_oh, s_hist_mm, s_hist, s_deg, s_rep = (sem(n) for n in ("s_hist_oh", "s_hist_mm", "s_hist", "s_deg", "s_rep"))
        s_clamped, s_sqrt, s_dblk = sem("s_clamped"), sem("s_sqrt"), sem("s_dblk")
        s_starts, s_starts_out, s_starts_in = sem("s_starts"), sem("s_starts_out"), sem("s_starts_in")
        s_bad, s_badsum = sem("s_bad"), sem("s_badsum")
        s_rowf, s_rowf_out = sem("s_rowf"), sem("s_rowf_out")
        s_match, s_look, s_picked, s_reduced, s_rows = (sem(n) for n in ("s_match", "s_look", "s_picked", "s_reduced", "s_rows"))
        s_rows_out = [sem("s_rows_out0"), sem("s_rows_out1")]
        s_factor, s_table, s_table_out, s_z = sem("s_factor"), sem("s_table"), sem("s_table_out"), sem("s_z")

        def edges_in(eng, tile, flat, count, signal):
            full, rest = count // EPP, count % EPP
            eng.dma_start(tile[0:full], flat[0:full * EPP].rearrange("(p e) -> p e", e=EPP)).then_inc(signal, 16)
            eng.dma_start(tile[full:full + 1, 0:rest], flat[full * EPP:count].unsqueeze(0)).then_inc(signal, 16)

        with nc.Block() as block:
            @block.gpsimd
            def _(pool):
                nc.gpsimd.memset(dst_i, PAD_DST)
                nc.gpsimd.memset(src_i, 0)
                nc.gpsimd.memset(next_i, PAD_DST)
                nc.gpsimd.memset(attr, 0.0).then_inc(s_pads, 1)
                nc.gpsimd.iota(iota_row[:, :], [[1, CH]], base=0, channel_multiplier=0,
                               allow_small_or_imprecise_dtypes=True)
                nc.gpsimd.iota(lanes, [[0, 1]], base=0, channel_multiplier=1, allow_small_or_imprecise_dtypes=True)
                nc.gpsimd.iota(steps5, [[WIN, 5]], base=0, channel_multiplier=0, allow_small_or_imprecise_dtypes=True)
                nc.gpsimd.iota(win_node[:, :], [[WIN, NW]], base=0, channel_multiplier=0,
                               allow_small_or_imprecise_dtypes=True)
                nc.gpsimd.iota(win_key[:, :], [[WKEYS, NW]], base=0, channel_multiplier=0,
                               allow_small_or_imprecise_dtypes=True).then_inc(s_iota, 1)
                nc.gpsimd.memset(zeros16[:, :], 0.0)
                nc.gpsimd.memset(ident[:, :], 0.0).then_inc(s_ident0, 1)
                pool.wait_ge(s_ident0, 1)
                nc.gpsimd.affine_select(out=ident[:, :], in_=ident[:, :], compare_op=ALU.not_equal, fill=1.0,
                                        base=0, pattern=[[-1, P]], channel_multiplier=1).then_inc(s_ident, 1)

            @block.sync
            def _(sp):
                sp.wait_ge(s_pads, 1)
                edges_in(sp, dst_i, dst, E, s_dst)
                edges_in(sp, src_i, src, E, s_src)
                edges_in(sp, next_i, dst[1:E], E - 1, s_next)
                sp.dma_start(attr[0:ROWS], edge_attr[0:ROWS * EPP, :].rearrange("(p e) k -> p e k", e=EPP)
                             ).then_inc(s_attr, 16)
                sp.dma_start(attr[ROWS:ROWS + 1, 0:REST], edge_attr[ROWS * EPP:E, :].unsqueeze(0)).then_inc(s_attr, 16)
                sp.wait_ge(s_codes, 1)
                sp.dma_start(src_lo_dram.rearrange("(p e) -> p e", e=EPP), src_lo).then_inc(s_codes_out, 16)
                sp.dma_start(src_hi_dram.rearrange("(p e) -> p e", e=EPP), src_hi).then_inc(s_codes_out, 16)
                sp.wait_ge(s_codes_out, 32)
                for g in range(GRP):
                    sp.dma_start(lo_bc[g * LO:(g + 1) * LO],
                                 src_lo_dram[g * HALF:(g + 1) * HALF].partition_broadcast(LO)).then_inc(s_bc, 16)
                    sp.dma_start(hi_bc[g * HI:(g + 1) * HI],
                                 src_hi_dram[g * HALF:(g + 1) * HALF].partition_broadcast(HI)).then_inc(s_bc, 16)
                sp.wait_ge(s_starts, 1)
                sp.dma_start(starts_dram.rearrange("(h q) -> q h", q=WQ), starts_i[0:WQ]).then_inc(s_starts_out, 16)
                sp.wait_ge(s_rowf, 1)
                sp.dma_start(dst_factor_dram.rearrange("(h l) -> l h", l=LO), t3[0:LO]).then_inc(s_rowf_out, 16)
                sp.wait_ge(s_starts_out, 16)
                sp.dma_start(starts_row[:, :], starts_dram.unsqueeze(0)).then_inc(s_starts_in, 16)
                with sp.Fori(0, LSTEPS // 8) as k:
                    for b in range(2):
                        sp.wait_ge(s_rows, k * 8 + 4 * b + 4)
                        sp.dma_start(src_factor_dram.rearrange("(g s n) -> g s n", g=GRP, n=4 * LC)
                                     [:, bass.ds(2 * k + b, 1), :].rearrange("g s n -> g (s n)"),
                                     factor_rows[0:GRP, b, :]).then_inc(s_rows_out[b], 16)
                for b in range(2):
                    sp.wait_ge(s_rows_out[b], 16 * (LSTEPS // 8))
                sp.dma_start(src_factor, src_factor_dram.rearrange("(p e) -> p e", e=EPP)).then_inc(s_factor, 16)
                sp.wait_ge(s_table, 1)
                sp.dma_start(edge_table.rearrange("(p e) w -> p (e w)", e=EPP),
                             table_tile.rearrange("p e w -> p (e w)")).then_inc(s_table_out, 16)
                sp.wait_ge(s_starts_in, 16)
                sp.wait_ge(s_rowf_out, 16)
                sp.wait_ge(s_table_out, 16)

            @block.vector
            def _(dve):
                steps = [0]

                def link(ins):
                    steps[0] += 1
                    ins.then_inc(s_dve1, 1)
                    dve.wait_ge(s_dve1, steps[0])

                dve.wait_ge(s_pads, 1)
                dve.wait_ge(s_iota, 1)
                link(nc.vector.memset(table_tile, 0.0))
                dve.wait_ge(s_dst, 32)
                link(nc.vector.tensor_copy(dst_f, dst_i))
                link(nc.vector.tensor_scalar(tmp_i, dst_i, LO - 1, None, ALU.bitwise_and))
                link(nc.vector.tensor_copy(dst_lo, tmp_i))
                link(nc.vector.tensor_scalar(tmp_i, dst_i, 6, None, ALU.logical_shift_right))
                link(nc.vector.tensor_copy(dst_hi, tmp_i))
                def hist(t0, b):
                    nc.vector.tensor_tensor(
                        oh_lo[:, b], iota_row[:, 0:LO].unsqueeze(1).broadcast_to([P, HCH, LO]),
                        dst_lo[:, bass.ds(t0, HCH)].unsqueeze(2).broadcast_to([P, HCH, LO]), ALU.is_equal)
                    nc.vector.tensor_tensor(
                        oh_hi[:, b], iota_row[:, 0:HI].unsqueeze(1).broadcast_to([P, HCH, HI]),
                        dst_hi[:, bass.ds(t0, HCH)].unsqueeze(2).broadcast_to([P, HCH, HI]), ALU.is_equal
                    ).then_inc(s_hist_oh, 1)
                for b in range(2):
                    hist(b * HCH, b)
                with dve.Fori(1, HSTEPS // 2) as k:
                    for b in range(2):
                        dve.wait_ge(s_hist_mm, 2 * k + b - 1)
                        hist((2 * k + b) * HCH, b)
                dve.wait_ge(s_src, 32)
                link(nc.vector.tensor_copy(src_f, src_i))
                link(nc.vector.tensor_scalar(tmp_i, src_i, LO - 1, None, ALU.bitwise_and))
                link(nc.vector.tensor_copy(src_lo, tmp_i))
                link(nc.vector.tensor_scalar(tmp_i, src_i, 6, None, ALU.logical_shift_right))
                nc.vector.tensor_copy(src_hi, tmp_i).then_inc(s_codes, 1)
                dve.wait_ge(s_codes, 1)
                link(nc.vector.tensor_scalar(tmp_i, src_i, P - 1, None, ALU.bitwise_and))
                link(nc.vector.tensor_copy(table_tile[:, :, 1], tmp_i))
                link(nc.vector.tensor_scalar(tmp_i, src_i, 7, None, ALU.logical_shift_right))
                link(nc.vector.scalar_tensor_tensor(table_tile[:, :, 0], dst_f, float(BLOCKS), tmp_i, ALU.mult, ALU.add))
                link(nc.vector.tensor_copy(table_tile[:, :, 2], dst_f))
                dve.wait_ge(s_next, 32)
                link(nc.vector.tensor_tensor(disorder, dst_i, next_i, ALU.is_gt))
                link(nc.vector.reduce_sum(bad, disorder, AX.X))
                nc.vector.memset(ones_t, 1.0)
                nc.vector.memset(ones1, 1.0)
                nc.vector.memset(dblk, 0.0)
                nc.vector.memset(dcol[:, :], 0.0)
                link(nc.vector.tensor_scalar(group_of[:, 1:2], lanes, float(HI), None, ALU.is_ge))
                nc.vector.tensor_scalar(group_of[:, 0:1], group_of[:, 1:2], -1.0, 1.0, ALU.mult, ALU.add)
                link(nc.vector.scalar_tensor_tensor(lane_hi, group_of[:, 1:2], -float(HI), lanes, ALU.mult, ALU.add))
                link(nc.vector.tensor_scalar(lane_lo, lanes, float(LO), None, ALU.is_ge))
                link(nc.vector.scalar_tensor_tensor(lane_lo, lane_lo, -float(LO), lanes, ALU.mult, ALU.add))
                link(nc.vector.tensor_scalar(below[0:LO], steps5[0:LO], lane_lo[0:LO], None, ALU.is_gt))
                link(nc.vector.tensor_tensor(within[0:LO], below[0:LO, 1:5], below[0:LO, 0:4], ALU.subtract))
                dve.wait_ge(s_ident, 1)
                nc.vector.tensor_copy(twice[0:LO, 0:LO], ident[0:LO, 0:LO])
                link(nc.vector.tensor_copy(twice[0:LO, LO:P], ident[0:LO, 0:LO]))
                dve.wait_ge(s_hist, 1)
                nc.vector.tensor_copy(t3[0:LO], banks[0][0:LO, 0:HI]).then_inc(s_deg, 1)
                dve.wait_ge(s_rep, 1)
                link(nc.vector.tensor_copy(deg, banks[1][:, 0:HI]))
                link(nc.vector.tensor_tensor_scan(t1[0:WQ], ones_t[0:WQ], banks[2][0:WQ, 0:HI], 0.0, ALU.mult, ALU.add))
                link(nc.vector.tensor_tensor(t1[0:WQ], t1[0:WQ], banks[2][0:WQ, 0:HI], ALU.subtract))
                link(nc.vector.tensor_tensor(t1[0:WQ], t1[0:WQ], banks[3][0:WQ, 0:HI], ALU.add))
                nc.vector.tensor_copy(starts_i[0:WQ], t1[0:WQ]).then_inc(s_starts, 1)
                link(nc.vector.tensor_scalar(t2[0:WQ], banks[4][0:WQ, 0:HI], float(CAP), None, ALU.is_gt))
                link(nc.vector.reduce_sum(bad4[0:WQ], t2[0:WQ], AX.X))
                link(nc.vector.tensor_tensor(bad[0:WQ], bad[0:WQ], bad4[0:WQ], ALU.add))
                nc.vector.tensor_copy(bad, bad).then_inc(s_bad, 1)
                nc.vector.tensor_scalar(t1, deg, 1.0, None, ALU.max).then_inc(s_clamped, 1)
                dve.wait_ge(s_clamped, 1)
                dve.wait_ge(s_sqrt, 1)
                link(nc.vector.reciprocal(dinv, t2))
                link(nc.vector.tensor_tensor(t3, dinv, dinv, ALU.mult))
                link(nc.vector.tensor_tensor(t3, t3, t1, ALU.mult))
                link(nc.vector.tensor_scalar(t3, t3, -0.5, 1.5, ALU.mult, ALU.add))
                link(nc.vector.tensor_tensor(dinv, dinv, t3, ALU.mult))
                link(nc.vector.tensor_scalar(t3, deg, 0.0, None, ALU.is_gt))
                link(nc.vector.tensor_tensor(dinv, dinv, t3, ALU.mult))
                nc.vector.tensor_scalar(t3, dinv, 1.0 / HSCALE, None, ALU.mult).then_inc(s_rowf, 1)
                nc.vector.tensor_scalar(dcol[0:LO, 0:BLOCKS], dinv[0:LO, 0:HI:2], HSCALE, None, ALU.mult)
                nc.vector.tensor_scalar(dcol[LO:P, 0:BLOCKS - 1], dinv[LO:P, 1:HI:2], HSCALE, None, ALU.mult)
                link(nc.vector.tensor_scalar(t1, dinv, DSCALE, None, ALU.mult))
                for g in range(GRP):
                    r = slice(g * LO, (g + 1) * LO)
                    link(nc.vector.tensor_copy(dblk[r, 0, g * HI:(g + 1) * HI], t1[r]))
                    link(nc.vector.tensor_tensor(dblk[r, 1, g * HI:(g + 1) * HI], t1[r],
                                                 dblk[r, 0, g * HI:(g + 1) * HI], ALU.subtract))
                nc.vector.tensor_copy(t2, t1).then_inc(s_dblk, 1)
                dve.wait_ge(s_badsum, 1)
                nc.vector.tensor_copy(flag_row[:, :], banks[5][0:1, 0:1])
                dve.wait_ge(s_bc, 16 * 2 * GRP)
                with dve.Fori(0, 7) as k:
                    part = lo_bc[:, bass.ds(k * (HALF // 7), HALF // 7)]
                    nc.vector.tensor_scalar(part, part, lane_lo, None, ALU.is_equal).then_inc(s_match, 1)
                with dve.Fori(0, LSTEPS // 8) as k:
                    for j in range(8):
                        n = k * 8 + j
                        dve.wait_ge(s_look, n + 1)
                        dve.wait_ge(s_reduced, n + 1)
                        nc.vector.scalar_tensor_tensor(
                            picked[0:GRP * HI, j % 2], hi_bc[0:GRP * HI, bass.ds(n * LC, LC)], lane_hi[0:GRP * HI],
                            banks[j % 2][0:GRP * HI, 0:LC], ALU.is_equal, ALU.mult).then_inc(s_picked, 1)
                dve.wait_ge(s_attr, 32)
                dve.wait_ge(s_factor, 16)
                link(nc.vector.tensor_tensor(attr, attr, src_factor.unsqueeze(2).broadcast_to([P, EPP, K_ATTR]), ALU.mult))
                link(nc.vector.tensor_copy(attr16[:, :, 0:K_ATTR], attr))
                link(nc.vector.tensor_tensor(attr16[:, :, K_ATTR:2 * K_ATTR], attr, attr16[:, :, 0:K_ATTR], ALU.subtract))
                nc.vector.tensor_copy(table_tile[:, :, 4:8], attr16.bitcast(f32)).then_inc(s_table, 1)

            @block.scalar
            def _(act):
                act.wait_ge(s_clamped, 1)
                nc.scalar.activation(t2, t1, ACT.Sqrt).then_inc(s_sqrt, 1)

                def rows(k, first):
                    for j in range(8):
                        if j % 4 == 0 and not first:
                            act.wait_ge(s_rows_out[j // 4], k * 16)
                        act.wait_ge(s_reduced, k * 8 + j + 3)
                        nc.scalar.copy(factor_rows[0:GRP, j // 4, (j % 4) * LC:(j % 4 + 1) * LC],
                                       banks[2 + j % 2][0:GRP, 0:LC]).then_inc(s_rows, 1)
                rows(0, True)
                with act.Fori(1, LSTEPS // 8) as k:
                    rows(k, False)

            @block.tensor
            def _(pe):
                pe.wait_ge(s_ident, 1)
                nc.tensor.matmul(banks[0][0:LO, 0:HI], zeros16[:, 0:LO], zeros16[:, 0:HI], start=True, stop=False)
                with pe.Fori(0, HSTEPS // 2) as k:
                    for b in range(2):
                        pe.wait_ge(s_hist_oh, 2 * k + b + 1)
                        for t in range(HCH):
                            last = nc.tensor.matmul(banks[0][0:LO, 0:HI], oh_lo[:, b, t, :], oh_hi[:, b, t, :],
                                                    start=False, stop=False)
                        last.then_inc(s_hist_mm, 1)
                nc.tensor.matmul(banks[0][0:LO, 0:HI], zeros16[:, 0:LO], zeros16[:, 0:HI], start=False,
                                 stop=True).then_inc(s_hist, 1)
                pe.wait_ge(s_deg, 1)
                nc.tensor.matmul(banks[1][:, 0:HI], twice[0:LO, :], t3[0:LO], start=True, stop=True)
                nc.tensor.matmul(banks[2][0:WQ, 0:HI], below[0:LO, 4:5].broadcast_to([LO, WQ]), t3[0:LO], start=True, stop=True)
                nc.tensor.matmul(banks[3][0:WQ, 0:HI], below[0:LO, 0:WQ], t3[0:LO], start=True, stop=True)
                nc.tensor.matmul(banks[4][0:WQ, 0:HI], within[0:LO], t3[0:LO], start=True, stop=True).then_inc(s_rep, 1)
                pe.wait_ge(s_bad, 1)
                nc.tensor.matmul(banks[5][0:1, 0:1], bad, ones1, start=True, stop=True).then_inc(s_badsum, 1)
                pe.wait_ge(s_dblk, 1)
                pe.wait_ge(s_match, 7)
                pe.sem_inc(s_reduced, 2)

                def look(n, j):
                    if j >= 2:
                        pe.wait_ge(s_picked, n - 1)
                    for s in range(2):
                        last = nc.tensor.matmul(banks[j % 2][0:GRP * HI, 0:LC], dblk[:, s, 0:GRP * HI],
                                                lo_bc[:, bass.ds(n * LC, LC)], start=(s == 0), stop=(s == 1))
                    last.then_inc(s_look, 1)

                with pe.Fori(0, LSTEPS // 8) as k:
                    look(k * 8, 0)
                    for j in range(8):
                        if j < 7:
                            look(k * 8 + j + 1, j + 1)
                        pe.wait_ge(s_picked, k * 8 + j + 1)
                        if j >= 2:
                            pe.wait_ge(s_rows, k * 8 + j - 1)
                        nc.tensor.matmul(banks[2 + j % 2][0:GRP, 0:LC], group_of[0:GRP * HI], picked[0:GRP * HI, j % 2],
                                         start=True, stop=True).then_inc(s_reduced, 1)
                    pe.wait_ge(s_rows, k * 8 + 8)

        s_edges = [sem(f"s_edges{j}") for j in range(UN)]
        s_onehots, s_window, s_taken = sem("s_onehots"), sem("s_window"), sem("s_taken")
        s_all_oh, s_all_mm, s_all_block, s_all_taken = (sem(n) for n in ("s_all_oh", "s_all_mm", "s_all_block", "s_all_taken"))
        s_sums, s_part, s_parts_in = sem("s_sums"), sem("s_part"), sem("s_parts_in")

        with nc.Block() as block:
            @block.sync
            def _(sp):
                irregular = sp.value_load(flag_row[0:1, 0:1])
                with sp.If(irregular > 0):
                    sp.nop()
                with sp.Else():
                    def fetch(k, first):
                        for j in range(UN):
                            w = UN * k + j
                            start = sp.value_load(starts_row[0:1, bass.ds(w, 1)], min_val=0, max_val=E)
                            if not first:
                                sp.wait_ge(s_window, w - UN + 1)
                            sp.dma_start(edge_buf[:, j].rearrange("p k w -> p (k w)"),
                                         edge_table[bass.ds(start, CAP), :].rearrange("(p k) w -> p (k w)", k=WT)
                                         ).then_inc(s_edges[j], 16)
                    fetch(0, True)
                    with sp.Fori(1, NW // UN) as k:
                        fetch(k, False)
                sp.wait_ge(s_part, 2)
                for s in range(2):
                    r = LO + K_ATTR * s
                    sp.dma_start(counts3[r:r + K_ATTR, BLOCKS - 1, :], attr_parts[:, s, :]).then_inc(s_parts_in, 16)
                sp.wait_ge(s_parts_in, 32)

            @block.vector
            def _(dve):
                irregular = dve.value_load(flag_row[0:1, 0:1])
                with dve.If(irregular > 0):
                    def all_edges(first, t, node0):
                        dve.wait_ge(s_all_mm, first)
                        for c in range(NCH):
                            last = nc.vector.tensor_scalar(all_dst[:, c * CH:(c + 1) * CH], iota_row[:, :], float(c * CH),
                                                           dst_f[:, bass.ds(t, 1)], ALU.add, ALU.is_equal)
                        if node0 is not None:
                            last = nc.vector.tensor_scalar(all_src, iota_row[:, 0:P], node0,
                                                           src_f[:, bass.ds(t, 1)], ALU.add, ALU.is_equal)
                        last.then_inc(s_all_oh, 1)
                    with dve.Fori(0, BLOCKS) as a:
                        with dve.Fori(0, EPP) as t:
                            all_edges(a * EPP + t + 1, t, win_node[:, bass.ds(a * (P // WIN), 1)])
                    with dve.Fori(0, EPP) as t:
                        all_edges(BLOCKS * EPP + t + 1, t, None)
                with dve.Else():
                    def onehots(k, first):
                        for j in range(UN):
                            w = UN * k + j
                            b = j % 2
                            dve.wait_ge(s_edges[j], 16 * k + 16)
                            if not (first and j < 2):
                                dve.wait_ge(s_window, w - 1)
                            for t in range(WT):
                                nc.vector.tensor_scalar(oh_key[:, b, t, :], iota_row[:, 0:WKEYS], win_key[:, bass.ds(w, 1)],
                                                        edge_buf[:, j, t, 0:1], ALU.add, ALU.is_equal)
                                nc.vector.tensor_scalar(oh_src[:, b, t, :], iota_row[:, 0:P], edge_buf[:, j, t, 1:2],
                                                        None, ALU.is_equal)
                                last = nc.vector.tensor_scalar(oh_dst[:, b, t, :], iota_row[:, 0:WIN],
                                                               win_node[:, bass.ds(w, 1)], edge_buf[:, j, t, 2:3],
                                                               ALU.add, ALU.is_equal)
                            last.then_inc(s_onehots, 1)
                    onehots(0, True)
                    with dve.Fori(1, NW // UN) as k:
                        onehots(k, False)
                dve.wait_ge(s_sums, 1)
                nc.vector.tensor_copy(attr_parts[:, 0, :], attr_sums).then_inc(s_part, 1)
                dve.wait_ge(s_part, 1)
                nc.vector.tensor_tensor(attr_parts[:, 1, :], attr_sums, attr_parts[:, 0, :], ALU.subtract).then_inc(s_part, 1)

            @block.tensor
            def _(pe):
                irregular = pe.value_load(flag_row[0:1, 0:1])
                with pe.If(irregular > 0):
                    def all_edges(base, lhsT, rows):
                        for c in range(NCH):
                            nc.tensor.matmul(banks[c][0:rows, 0:CH], zeros16[:, 0:rows], zeros16[:, :], start=True, stop=False)
                        with pe.Fori(0, EPP) as t:
                            pe.wait_ge(s_all_oh, base + t + 1)
                            parts = lhsT(t)
                            for w in parts:
                                for c in range(NCH):
                                    last = nc.tensor.matmul(banks[c][0:rows, 0:CH], w, all_dst[:, c * CH:(c + 1) * CH],
                                                            start=False, stop=False)
                            last.then_inc(s_all_mm, 1)
                        for c in range(NCH):
                            last = nc.tensor.matmul(banks[c][0:rows, 0:CH], zeros16[:, 0:rows], zeros16[:, :], start=False, stop=True)
                        last.then_inc(s_all_block, 1)
                    pe.sem_inc(s_all_mm, 1)
                    with pe.Fori(0, BLOCKS) as a:
                        pe.wait_ge(s_all_taken, a + 1)
                        all_edges(a * EPP, lambda t: [all_src], P)
                    pe.wait_ge(s_all_taken, BLOCKS + 1)
                    all_edges(BLOCKS * EPP, lambda t: [attr16[:, bass.ds(t, 1), K_ATTR * s:K_ATTR * (s + 1)]
                                                       .rearrange("p o k -> p (o k)") for s in range(2)], K_ATTR)
                with pe.Else():
                    def products(k, first):
                        for j in range(UN):
                            w = UN * k + j
                            b = j % 2
                            pe.wait_ge(s_onehots, w + 1)
                            if not (first and j < 2):
                                pe.wait_ge(s_taken, w - 1)
                            for t in range(WT):
                                nc.tensor.matmul(banks[b][:, 0:WKEYS], oh_src[:, b, t, :], oh_key[:, b, t, :],
                                                 start=(t == 0), stop=(t == WT - 1))
                            for t in range(WT):
                                a16 = edge_buf[:, j, t, 4:8].bitcast(f16)
                                for s in range(2):
                                    last = nc.tensor.matmul(banks[2 + b][0:K_ATTR, 0:WIN], a16[:, K_ATTR * s:K_ATTR * (s + 1)],
                                                            oh_dst[:, b, t, :], start=(t == 0 and s == 0),
                                                            stop=(t == WT - 1 and s == 1))
                            last.then_inc(s_window, 1)
                    products(0, True)
                    with pe.Fori(1, NW // UN) as k:
                        products(k, False)

            @block.scalar
            def _(act):
                irregular = act.value_load(flag_row[0:1, 0:1])
                with act.If(irregular > 0):
                    act.sem_inc(s_all_taken, 1)
                    with act.Fori(0, BLOCKS) as a:
                        act.wait_ge(s_all_block, a + 1)
                        for c in range(NCH):
                            last = nc.scalar.copy(countsT[:, bass.ds(a * NP + c * CH, CH)], banks[c][:, 0:CH])
                        last.then_inc(s_all_taken, 1)
                    act.wait_ge(s_all_block, BLOCKS + 1)
                    for c in range(NCH):
                        last = nc.scalar.mul(attr_sums[:, c * CH:(c + 1) * CH], banks[c][0:K_ATTR, 0:CH], 1.0 / DSCALE)
                    last.then_inc(s_sums, 1)
                with act.Else():
                    with act.Fori(0, NW // UN) as k:
                        for j in range(UN):
                            w = UN * k + j
                            act.wait_ge(s_window, w + 1)
                            nc.scalar.copy(counts3[:, :, bass.ds(w * WIN, WIN)],
                                           banks[j % 2][:, 0:WKEYS].rearrange("p (d a) -> p a d", a=BLOCKS))
                            nc.scalar.mul(attr_sums[:, bass.ds(w * WIN, WIN)], banks[2 + j % 2][0:K_ATTR, 0:WIN],
                                          1.0 / DSCALE).then_inc(s_taken, 1)
                    act.wait_ge(s_taken, NW)
                    act.sem_inc(s_sums, 1)

        s_x, s_aff, s_h, s_lnz = sem("s_x"), sem("s_aff"), sem("s_h"), sem("s_lnz")
        s_chain, s_var, s_root, s_ln, s_h0 = (sem(n) for n in ("s_chain", "s_var", "s_root", "s_ln", "s_h0"))
        s_h0T, s_norm, s_tr, s_hi, s_parts = (sem(n) for n in ("s_h0T", "s_norm", "s_tr", "s_hi", "s_parts"))
        s_ew, s_ewhi, s_ewparts, s_w, s_df = (sem(n) for n in ("s_ew", "s_ewhi", "s_ewparts", "s_w", "s_df"))
        s_sum = [sem("s_sum0"), sem("s_sum1")]
        s_agg = [sem("s_agg0"), sem("s_agg1")]
        s_mlp, s_relu, s_bnvar, s_bnroot, s_affine = (sem(n) for n in ("s_mlp", "s_relu", "s_bnvar", "s_bnroot", "s_affine"))
        s_xr, s_res, s_out = sem("s_xr"), sem("s_res"), sem("s_out")

        mean_var = mv_a[:, :].rearrange("p (i v) -> p i v", v=2)
        ln_v, ln_r, ln_t, ln_b = (mv[:, BLOCKS * n:BLOCKS * (n + 1)] for n in range(4))
        stats4 = stats[:, :].rearrange("p (f c s) -> p f c s", f=HALVES, s=6)
        ln_stats = work[:, 0:6 * BLOCKS].rearrange("p (i s) -> p i s", s=6)
        bn_mv = small[:, 0:4].rearrange("p (f v) -> p f v", f=HALVES)
        bn_v, bn_r, bn_t, bn_scale, bn_shift = (small[:, 4 + 2 * n:6 + 2 * n] for n in range(5))
        EWR = slice(LO, LO + 2 * K_ATTR)
        x_again = countsT[:, 0:2 * BLOCKS * D].bitcast(f32).rearrange("p (i f) -> p i f", i=BLOCKS)
        out_tiles = countsT[:, 2 * BLOCKS * D:4 * BLOCKS * D].bitcast(f32).rearrange("p (i f) -> p i f", i=BLOCKS)

        def nodes(i):
            return P if i < BLOCKS - 1 else TAIL

        with nc.Block() as block:
            @block.sync
            def _(sp):
                sp.dma_start(x_tiles[:, 0:BLOCKS - 1], x[0:(BLOCKS - 1) * P, :].rearrange("(i p) f -> p i f", p=P)).then_inc(s_x, 16)
                sp.dma_start(x_tiles[0:TAIL, BLOCKS - 1], x[(BLOCKS - 1) * P:N, :]).then_inc(s_x, 16)
                for n, v in enumerate((mlp_b, bn_g, bn_b)):
                    sp.dma_start(aff[:, n, :], v.rearrange("l (f p) -> p (l f)", p=P)).then_inc(s_aff, 16)
                sp.wait_ge(s_lnz, 1)

                def layer(l):
                    sp.wait_ge(s_mlp, l * NCH + 1)
                    sp.dma_start(weights, mlp_w[bass.ds(l, 1)].rearrange("l (k p) n -> p (l k) n", p=P)).then_inc(s_w, 16)
                    sp.wait_ge(s_ewparts, l + 1)
                    for s in range(2):
                        r = LO + K_ATTR * s
                        sp.dma_start(ewt[r:r + 3, P:D], ew2[bass.ds(l, 1)].rearrange("l k n -> (l k) n")).then_inc(s_ew, 16)
                        sp.dma_start(ewt[r + 3:r + 4, 0:P], ew1[bass.ds(l, 1)].rearrange("l k n -> (l k) n")).then_inc(s_ew, 16)
                    with sp.Fori(0, NCH) as c:
                        sp.wait_ge(s_agg[1], l * NCH + c + 1)
                        sp.dma_start(dst_factor, dst_factor_dram[bass.ds(c * CH, CH)].partition_broadcast(P)).then_inc(s_df, 16)
                with sp.Fori(0, L - 1) as l:
                    layer(l)
                layer(L - 1)
                sp.wait_ge(s_mlp, L * NCH + 1)
                sp.dma_start(x_again[:, 0:BLOCKS - 1], x[0:(BLOCKS - 1) * P, :].rearrange("(i p) f -> p i f", p=P)).then_inc(s_xr, 16)
                sp.dma_start(x_again[0:TAIL, BLOCKS - 1], x[(BLOCKS - 1) * P:N, :]).then_inc(s_xr, 16)
                for g in range(NBQ):
                    i0, i1 = g * BQ, (g + 1) * BQ
                    sp.wait_ge(s_res, i1)
                    if i1 == BLOCKS:
                        i1 -= 1
                        sp.dma_start(out[i1 * P:N, :], out_tiles[0:TAIL, i1]).then_inc(s_out, 16)
                    sp.dma_start(out[i0 * P:i1 * P, :].rearrange("(i p) f -> p i f", p=P), out_tiles[:, i0:i1]).then_inc(s_out, 16)
                sp.wait_ge(s_out, 16 * (NBQ + 1))

            @block.gpsimd
            def _(pool):
                nc.gpsimd.memset(ewt[:, :], 0.0).then_inc(s_ewparts, 1)

            @block.vector
            def _(dve):
                steps = [0]

                def link(ins):
                    steps[0] += 1
                    ins.then_inc(s_chain, 1)
                    dve.wait_ge(s_chain, steps[0])

                def newton(v, r, t, chain):
                    chain(nc.vector.reciprocal(r, r))
                    chain(nc.vector.tensor_tensor(t, r, r, ALU.mult))
                    chain(nc.vector.tensor_tensor(t, t, v, ALU.mult))
                    chain(nc.vector.tensor_scalar(t, t, -0.5, 1.5, ALU.mult, ALU.add))
                    chain(nc.vector.tensor_tensor(r, r, t, ALU.mult))

                link(nc.vector.memset(mv_a[:, :], 0.0))
                dve.wait_ge(s_x, 32)
                for i in range(BLOCKS):
                    last = nc.vector.bn_stats(ln_stats[0:nodes(i), i], x_tiles[0:nodes(i), i])
                link(last)
                for i in range(BLOCKS):
                    last = nc.vector.bn_aggr(mean_var[0:nodes(i), i], ln_stats[0:nodes(i), i])
                link(last)
                dve.sem_inc(s_lnz, 1)
                nc.vector.tensor_scalar(ln_v, mean_var[:, :, 1], EPS, None, ALU.add).then_inc(s_var, 1)
                dve.wait_ge(s_var, 1)
                dve.wait_ge(s_root, 1)
                newton(ln_v, ln_r, ln_t, link)
                nc.vector.scalar_tensor_tensor(ln_b, mean_var[:, :, 0], -1.0, ln_r, ALU.mult, ALU.mult).then_inc(s_ln, 1)
                nc.vector.memset(hT3[:, :, N:NP], 0.0)
                for i in range(BLOCKS):
                    dve.wait_ge(s_h0T, i + 1)
                    last = nc.vector.tensor_copy(hT3[:, :, i * P:i * P + nodes(i)],
                                                 banks[4 + i % 2][:, 0:D].rearrange("p (f n) -> p f n", f=HALVES)[:, :, 0:nodes(i)])
                    last.then_inc(s_h0, 1)
                dve.wait_ge(s_h0, BLOCKS)
                dve.sem_inc(s_norm, NBQ)
                nc.vector.memset(hs4[:, BLOCKS - 1], 0.0).then_inc(s_lnz, 1)
                for h in range(2):
                    dve.sem_inc(s_agg[h], 1)
                base = steps[0]
                CHAIN = 11

                def layer(l):
                    dve.wait_ge(s_ewhi, l + 1)
                    nc.vector.scalar_tensor_tensor(hs4[EWR, BLOCKS - 1, 1], ewt[EWR, :], HSCALE, hs4[EWR, BLOCKS - 1, 0],
                                                   ALU.mult, ALU.subtract).then_inc(s_ewparts, 1)
                    for i in range(BLOCKS):
                        dve.wait_ge(s_hi, l * BLOCKS + i + 1)
                        n = nodes(i)
                        nc.vector.scalar_tensor_tensor(hs4[0:n, i, 1], banks[4 + i % 2][0:n, 0:D], dcol[0:n, i:i + 1],
                                                       hs4[0:n, i, 0], ALU.mult, ALU.subtract).then_inc(s_parts, 1)

                    def take(n, h):
                        dve.wait_ge(s_sum[h], n + 1)
                        dve.wait_ge(s_mlp, n + 1)
                        if h == 0:
                            dve.wait_ge(s_df, 16 * n + 16)
                        nc.vector.tensor_tensor(agg[:, h, :], banks[h][:, 0:CH], dst_factor, ALU.mult).then_inc(s_agg[h], 1)

                    def chunk_stats(n, c, size):
                        dve.wait_ge(s_relu, n + 2)
                        for f in range(HALVES):
                            last = nc.vector.bn_stats(stats4[:, f, c, :] if isinstance(c, int) else
                                                      stats4[:, f, bass.ds(c, 1), :].rearrange("p c s -> p (c s)"),
                                                      hT3[:, f, bass.ds(c * CH, size)])
                        return last
                    take(l * NCH, 0)
                    take(l * NCH, 1)
                    with dve.Fori(1, NCH) as c:
                        take(l * NCH + c, 0)
                        chunk_stats(l * NCH + c - 1, c - 1, CH)
                        take(l * NCH + c, 1)
                    count = [0]

                    def chain(ins):
                        count[0] += 1
                        ins.then_inc(s_chain, 1)
                        dve.wait_ge(s_chain, l * CHAIN + base + count[0])
                    chain(chunk_stats(l * NCH + NCH - 1, NCH - 1, LAST_CH))
                    nc.vector.memset(bn_shift, 0.0)
                    for f in range(HALVES):
                        last = nc.vector.bn_aggr(bn_mv[:, f], stats4[:, f].rearrange("p c s -> p (c s)"))
                    chain(last)
                    chain(nc.vector.tensor_scalar(bn_v, bn_mv[:, :, 1], EPS, None, ALU.add))
                    nc.vector.tensor_copy(bn_t, bn_v).then_inc(s_bnvar, 1)
                    dve.wait_ge(s_bnroot, l + 1)
                    newton(bn_v, bn_r, bn_t, chain)
                    cols = bass.ds(l * HALVES, HALVES)
                    chain(nc.vector.tensor_tensor(bn_scale, bn_r, aff[:, 1, cols], ALU.mult))
                    chain(nc.vector.tensor_tensor(bn_t, bn_mv[:, :, 0], bn_scale, ALU.mult))
                    chain(nc.vector.tensor_tensor(bn_shift, aff[:, 2, cols], bn_t, ALU.subtract))
                    assert count[0] == CHAIN, count
                    dve.sem_inc(s_affine, 1)

                dve.wait_ge(s_aff, 48)
                with dve.Fori(0, L - 1) as l:
                    layer(l)
                layer(L - 1)
                dve.wait_ge(s_xr, 32)
                for i in range(BLOCKS):
                    n = nodes(i)
                    dve.wait_ge(s_tr, L * BLOCKS + i + 1)
                    nc.vector.tensor_tensor(out_tiles[0:n, i], banks[4 + i % 2][0:n, 0:D], x_again[0:n, i], ALU.add).then_inc(s_res, 1)

            @block.scalar
            def _(act):
                act.wait_ge(s_var, 1)
                nc.scalar.activation(ln_r, ln_v, ACT.Sqrt).then_inc(s_root, 1)
                act.wait_ge(s_ln, 1)
                for i in range(BLOCKS):
                    n = nodes(i)
                    nc.scalar.activation(x_tiles[0:n, i], x_tiles[0:n, i], ACT.Relu, bias=ln_b[0:n, i:i + 1],
                                         scale=ln_r[0:n, i:i + 1]).then_inc(s_h, 1)
                act.wait_ge(s_lnz, 2)
                act.sem_inc(s_relu, 1)

                def layer(l):
                    act.wait_ge(s_ew, 64 * l + 64)
                    nc.scalar.mul(hs4[EWR, BLOCKS - 1, 0], ewt[EWR, :], HSCALE).then_inc(s_ewhi, 1)
                    for i in range(BLOCKS):
                        n = nodes(i)
                        act.wait_ge(s_tr, l * BLOCKS + i + 1)
                        nc.scalar.activation(hs4[0:n, i, 0], banks[4 + i % 2][0:n, 0:D], ACT.Copy,
                                             scale=dcol[0:n, i:i + 1]).then_inc(s_hi, 1)
                    with act.Fori(0, NCH) as c:
                        act.wait_ge(s_mlp, l * NCH + c + 2)
                        for f in range(HALVES):
                            last = nc.scalar.activation(hT3[:, f, bass.ds(c * CH, CH)], banks[2 + f][:, 0:CH], ACT.Relu,
                                                        bias=aff[:, 0, bass.ds(l * HALVES + f, 1)])
                        last.then_inc(s_relu, 1)
                    act.wait_ge(s_bnvar, l + 1)
                    nc.scalar.activation(bn_r, bn_v, ACT.Sqrt).then_inc(s_bnroot, 1)
                    act.wait_ge(s_affine, l + 1)

                def normalize(func):
                    for g in range(NBQ):
                        cols = slice(g * BQ * P, min((g + 1) * BQ * P, NP))
                        for f in range(HALVES):
                            last = nc.scalar.activation(hT3[:, f, cols], hT3[:, f, cols], func, bias=bn_shift[:, f:f + 1],
                                                        scale=bn_scale[:, f:f + 1])
                        last.then_inc(s_norm, 1)

                act.wait_ge(s_aff, 48)
                with act.Fori(0, L - 1) as l:
                    layer(l)
                    normalize(ACT.Relu)
                layer(L - 1)
                normalize(ACT.Identity)

            @block.tensor
            def _(pe):
                for i in range(BLOCKS):
                    n = nodes(i)
                    pe.wait_ge(s_h, i + 1)
                    if i >= 2:
                        pe.wait_ge(s_h0, i - 1)
                    for f in range(HALVES):
                        last = nc.tensor.transpose(banks[4 + i % 2][:, f * P:f * P + n], x_tiles[0:n, i, f * P:(f + 1) * P],
                                                   ident[0:n, 0:n])
                    last.then_inc(s_h0T, 1)
                pe.sem_inc(s_mlp, 1)

                def transposes(l, ready):
                    for i in range(BLOCKS):
                        n = nodes(i)
                        if i % BQ == 0:
                            pe.wait_ge(s_norm, l * NBQ + i // BQ + 1)
                        if 2 <= i < BLOCKS - 1:
                            pe.wait_ge(ready, (l * BLOCKS if ready is s_parts else 0) + i - 1 + (i == BLOCKS - 2))
                        for f in range(HALVES):
                            last = nc.tensor.transpose(banks[4 + i % 2][0:n, f * P:(f + 1) * P],
                                                       hT3[:, f, i * P:i * P + n], ident[:, :])
                        last.then_inc(s_tr, 1)

                def layer(l):
                    transposes(l, s_parts)
                    pe.wait_ge(s_parts, l * BLOCKS + BLOCKS)
                    pe.wait_ge(s_ewparts, l + 2)

                    def sums(n, c, h):
                        pe.wait_ge(s_agg[h], n + 1)
                        for i in range(BLOCKS):
                            for s in range(2):
                                last = nc.tensor.matmul(banks[h][:, 0:CH], hs4[:, i, s, h * P:(h + 1) * P],
                                                        countsT[:, bass.ds(c * CH + i * NP, CH)],
                                                        start=(i == 0 and s == 0), stop=(i == BLOCKS - 1 and s == 1))
                        last.then_inc(s_sum[h], 1)

                    def mlp(n, c):
                        pe.wait_ge(s_w, 16 * l + 16)
                        for h in range(2):
                            pe.wait_ge(s_agg[h], n + 2)
                        pe.wait_ge(s_relu, n + 1)
                        for f in range(HALVES):
                            for k in range(4):
                                rhs = hT3[:, k, bass.ds(c * CH, CH)] if k < 2 else agg[:, k - 2, :]
                                last = nc.tensor.matmul(banks[2 + f][:, 0:CH], weights[:, k, f * P:(f + 1) * P], rhs,
                                                        start=(k == 0), stop=(k == 3))
                        last.then_inc(s_mlp, 1)

                    sums(l * NCH, 0, 0)
                    sums(l * NCH, 0, 1)
                    with pe.Fori(1, NCH) as c:
                        sums(l * NCH + c, c, 0)
                        mlp(l * NCH + c - 1, c - 1)
                        sums(l * NCH + c, c, 1)
                    mlp(l * NCH + NCH - 1, NCH - 1)

                with pe.Fori(0, L - 1) as l:
                    layer(l)
                layer(L - 1)
                transposes(L, s_res)


_INS = ["x", "src", "dst", "edge_attr_4", "L0_gnn_mlp_w", "L0_gnn_mlp_b", "L0_gnn_ew1", "L0_gnn_ew2", "L0_gnn_bn_g", "L0_gnn_bn_b"]


def kernel(**inputs):
    import numpy as _np
    import concourse.bacc as _bacc
    from concourse import mybir as _mybir
    from concourse.bass_utils import run_bass_kernel_spmd as _run

    nc = _bacc.Bacc("TRN2", target_bir_lowering=False, num_devices=1, dynamic_dma_scratch_size=1024)
    arrays, args = {}, []
    for name in _INS:
        a = _np.ascontiguousarray(inputs[name])
        arrays[f"in_{name}"] = a
        args.append(nc.dram_tensor(f"in_{name}", a.shape, _mybir.dt.from_np(a.dtype), kind="ExternalInput").ap())
    shape = inputs["x"].shape
    args.append(nc.dram_tensor("out_0", shape, _mybir.dt.float32, kind="ExternalOutput").ap())
    gnn_program(nc, *args)
    r = _run(nc, [arrays], core_ids=[0])
    return r.results[0]["out_0"]
```

```python
import concourse.bass as bass
from concourse import mybir
from contextlib import ExitStack


def gnn_program(nc, x, src, dst, edge_attr, mlp_w, mlp_b, ew1, ew2, bn_g, bn_b, out):
    f32, f16, i32 = mybir.dt.float32, mybir.dt.float16, mybir.dt.int32
    ALU, ACT, AX = mybir.AluOpType, mybir.ActivationFunctionType, mybir.AxisListType

    P = 128
    N, D = x.shape
    E = src.shape[0]
    K_ATTR = edge_attr.shape[1]
    L = mlp_w.shape[0]
    HALVES = D // P
    BLOCKS = -(-N // P)
    TAIL = N - (BLOCKS - 1) * P
    LO, HI = 64, 49
    NP = LO * HI
    WIN = 16
    NW = NP // WIN
    WQ = LO // WIN
    WKEYS = BLOCKS * WIN
    WT = 3
    CAP = WT * P
    UN = 4
    CH = 448
    NCH = NP // CH
    LAST_CH = N - (NCH - 1) * CH
    EPP = 420
    EP = P * EPP
    ROWS = E // EPP
    REST = E - ROWS * EPP
    PAD_DST = 4000
    GRP = 2
    HALF = EP // GRP
    LT = 6
    LC = LO * LT
    LUN = 10
    LSTEPS = EPP // LT
    LDEEP = 5
    HCH = 42
    HSTEPS = EPP // HCH
    TW = 8
    DSCALE = 1024.0
    HSCALE = 256.0
    EPS = 1e-5
    BQ = 5
    NBQ = BLOCKS // BQ
    assert NP >= N and NP % CH == 0 and EP >= E + CAP and BLOCKS * P >= N and D == 2 * P
    assert HALF == LO * EPP and LSTEPS % LUN == 0 and LUN % LDEEP == 0 and LT % 2 == 0 and EPP % HCH == 0 and HSTEPS % 2 == 0 and NW % UN == 0 and NW // UN % 2 == 1
    assert BLOCKS % BQ == 0 and TAIL <= LO

    ctx = ExitStack()
    with ctx:
        ctx.enter_context(nc.allow_non_contiguous_dma(reason="short tables, once"))

        def sb(name, shape, dt):
            return ctx.enter_context(nc.sbuf_tensor(name, shape, dt))

        def sem(name):
            return ctx.enter_context(nc.semaphore(name))

        edge_table = nc.dram_tensor("edge_table", [EP, TW], f32).ap()
        src_lo_dram = nc.dram_tensor("src_lo_dram", [EP], f16).ap()
        src_hi_dram = nc.dram_tensor("src_hi_dram", [EP], f16).ap()
        dst_factor_dram = nc.dram_tensor("dst_factor_dram", [NP], f32).ap()
        starts_dram = nc.dram_tensor("starts_dram", [NW], i32).ap()

        countsT = sb("countsT", [P, BLOCKS * NP], f16)
        hT = sb("hT", [P, HALVES * NP], f32)
        hs = sb("hs", [P, BLOCKS * 2 * D], f16)
        work = sb("work", [P, 2816], f32)
        hT3 = hT[:, :].rearrange("p (f n) -> p f n", f=HALVES)
        hs4 = hs[:, :].rearrange("p (i s f) -> p i s f", i=BLOCKS, s=2)
        counts3 = countsT[:, :].rearrange("p (a n) -> p a n", a=BLOCKS)

        iota_row = sb("iota_row", [P, CH], f16)
        zeros16 = sb("zeros16", [P, CH], f16)
        ident = sb("ident", [P, P], f32)
        win_node = sb("win_node", [P, NW], f32)
        win_key = sb("win_key", [P, NW], f32)
        starts_row = sb("starts_row", [1, NW], i32)
        flag_row = sb("flag_row", [1, 1], i32)
        edge_buf = sb("edge_buf", [P, 2, UN, WT, TW], f32)
        dcol = sb("dcol", [P, BLOCKS], f32)
        ewt = sb("ewt", [P, D], f32)
        aff = sb("aff", [P, 3, L * HALVES], f32)
        stats = sb("stats", [P, HALVES * NCH * 6], f32)
        small = sb("small", [P, 24], f32)
        mv = sb("mv", [P, 4 * BLOCKS], f32)
        mv_a = sb("mv_a", [P, 2 * BLOCKS], f32)

        def early(lo, n, dt=f16):
            view = countsT[:, lo:lo + n]
            return view if dt == f16 else view.bitcast(dt)
        lo_bc = early(0, HALF)
        hi_bc = early(HALF, HALF)
        at = GRP * HALF
        oh_lo = early(at, 2 * HCH * LO).rearrange("p (b v t) -> p b v t", b=2, v=LO)
        oh_hi = early(at + 2 * HCH * LO, 2 * HCH * HI).rearrange("p (b v t) -> p b v t", b=2, v=HI)
        digit_of = early(at + 2 * HCH * (LO + HI), HCH * LO).rearrange("p (v t) -> p v t", v=LO)
        picked = early(at, LDEEP * 2 * LC, f32).rearrange("p (b t v) -> p b t v", b=LDEEP, v=LO)
        table_at = at + 2 * HCH * (LO + HI) + HCH * LO
        table_tile = early(table_at, 2 * EPP * TW, f32).rearrange("p (e w) -> p e w", w=TW)
        assert LDEEP * 2 * LC <= 2 * HCH * (LO + HI) and table_at + 2 * EPP * TW <= BLOCKS * NP
        lo_bc3 = lo_bc.rearrange("p (q t) -> p q t", t=EPP)
        hi_bc3 = hi_bc.rearrange("p (q t) -> p q t", t=EPP)

        hs_f = hs[:, :].bitcast(f32)
        src_f = hs_f[:, 0:EPP]
        dst_f = hs_f[:, EPP:2 * EPP]
        src_i = hs_f[:, 2 * EPP:3 * EPP].bitcast(i32)
        dst_i = hs_f[:, 3 * EPP:4 * EPP].bitcast(i32)
        tmp_i = hs_f[:, 4 * EPP:5 * EPP].bitcast(i32)
        next_i = hs_f[:, 5 * EPP:6 * EPP].bitcast(i32)
        attr16 = hs_f[:, 6 * EPP:10 * EPP].bitcast(f16).rearrange("p (e k) -> p e k", k=2 * K_ATTR)
        all_dst = hs_f[:, 10 * EPP:10 * EPP + NP // 2].bitcast(f16)
        all_src = hs_f[:, 10 * EPP + NP // 2:10 * EPP + NP // 2 + P // 2].bitcast(f16)
        x_tiles = hs_f[:, 0:BLOCKS * D].rearrange("p (i f) -> p i f", i=BLOCKS)

        attr = hT[:, 0:EPP * K_ATTR].rearrange("p (e k) -> p e k", k=K_ATTR)
        q = EPP * K_ATTR
        src_factor = hT[:, q:q + EPP]
        src_lo = hT[:, q + EPP:q + EPP + EPP // 2].bitcast(f16)
        src_hi = hT[:, q + EPP + EPP // 2:q + 2 * EPP].bitcast(f16)
        dst_lo = hT[:, q + 2 * EPP:q + 2 * EPP + EPP // 2].bitcast(f16)
        dst_hi = hT[:, q + 2 * EPP + EPP // 2:q + 3 * EPP].bitcast(f16)
        disorder = hT[:, q + 3 * EPP:q + 4 * EPP]
        q2 = q + 4 * EPP
        deg = hT[:, q2:q2 + HI]
        dinv = hT[:, q2 + 64:q2 + 64 + HI]
        t1 = hT[:, q2 + 128:q2 + 128 + HI]
        t2 = hT[:, q2 + 192:q2 + 192 + HI]
        t3 = hT[:, q2 + 256:q2 + 256 + HI]
        ones_t = hT[:, q2 + 320:q2 + 320 + HI]
        twice = hT[:, q2 + 384:q2 + 384 + P]
        group_of = hT[:, q2 + 512:q2 + 514]
        lanes = hT[:, q2 + 514:q2 + 515]
        lane_lo = hT[:, q2 + 515:q2 + 516]
        lane_hi = hT[:, q2 + 516:q2 + 517]
        steps5 = hT[:, q2 + 520:q2 + 525]
        below = hT[:, q2 + 530:q2 + 535]
        within = hT[:, q2 + 540:q2 + 544]
        bad = hT[:, q2 + 545:q2 + 546]
        bad4 = hT[:, q2 + 546:q2 + 547]
        ones1 = hT[:, q2 + 547:q2 + 548]
        starts_i = hT[:, q2 + 550:q2 + 550 + HI].bitcast(i32)
        dblk = hT[:, q2 + 600:q2 + 600 + P].bitcast(f16).rearrange("p (s c) -> p s c", s=2)
        assert q2 + 600 + P <= HALVES * NP
        attr_sums = hT[0:K_ATTR, 0:NP]
        attr_parts = hT[0:K_ATTR, NP:2 * NP].bitcast(f16).rearrange("p (s n) -> p s n", s=2)

        TILES = UN * WT
        wide = hT[:, NP:2 * NP].bitcast(f16)
        oh_src = wide[:, 0:2 * TILES * P].rearrange("p (b v n) -> p b v n", b=2, v=P)
        o = 2 * TILES * P
        oh_dst = wide[:, o:o + 2 * TILES * WIN].rearrange("p (b n v) -> p b n v", b=2, n=TILES)
        o += 2 * TILES * WIN
        lane16 = wide[:, o:o + 2 * TILES].rearrange("p (b n) -> p b n", b=2)
        o += 2 * TILES
        own_key = wide[:, o:o + 4 * TILES].bitcast(f32).rearrange("p (b n) -> p b n", b=2)
        o += 4 * TILES
        assert NP + o // 2 <= 2 * NP - (TILES * P + TILES * WIN) // 2
        lane_of = wide[:, 2 * NP - TILES * P:2 * NP].rearrange("p (v n) -> p v n", v=P)
        node_of = wide[:, 2 * NP - TILES * P - TILES * WIN:2 * NP - TILES * P]
        assert q2 + 600 + P <= 2 * NP - (TILES * P + TILES * WIN) // 2

        work16 = work[:, :].bitcast(f16)
        oh_key = work16[:, 0:UN * WT * WKEYS].rearrange("p (b k v) -> p b k v", b=UN, k=WT)
        weights = work[:, 0:4 * D].rearrange("p (k n) -> p k n", k=4)
        agg = work[:, 4 * D:4 * D + 2 * CH].rearrange("p (f n) -> p f n", f=HALVES)
        dst_factor = work[:, 4 * D + 2 * CH:4 * D + 3 * CH]

        banks = [ctx.enter_context(nc.psum_tensor(f"bank{n}", [P, 512], f32)) for n in range(8)]
        look_banks = banks[0:2] + banks[3:3 + LDEEP - 2]

        s_pads, s_src, s_dst, s_next, s_attr = (sem(n) for n in ("s_pads", "s_src", "s_dst", "s_next", "s_attr"))
        s_iota, s_ident0, s_ident = sem("s_iota"), sem("s_ident0"), sem("s_ident")
        s_dve1, s_codes, s_codes_out, s_bc = sem("s_dve1"), sem("s_codes"), sem("s_codes_out"), sem("s_bc")
        s_hist_oh, s_hist_mm, s_hist, s_deg, s_rep = (sem(n) for n in ("s_hist_oh", "s_hist_mm", "s_hist", "s_deg", "s_rep"))
        s_clamped, s_sqrt, s_dblk = sem("s_clamped"), sem("s_sqrt"), sem("s_dblk")
        s_starts, s_starts_out, s_starts_in = sem("s_starts"), sem("s_starts_out"), sem("s_starts_in")
        s_bad, s_badsum = sem("s_bad"), sem("s_badsum")
        s_rowf, s_rowf_out = sem("s_rowf"), sem("s_rowf_out")
        s_match, s_look, s_picked, s_reduced = (sem(n) for n in ("s_match", "s_look", "s_picked", "s_reduced"))
        s_pads2, s_table, s_table_out = sem("s_pads2"), sem("s_table"), sem("s_table_out")

        def edges_in(eng, tile, flat, count, signal):
            full, rest = count // EPP, count % EPP
            eng.dma_start(tile[0:full], flat[0:full * EPP].rearrange("(p e) -> p e", e=EPP)).then_inc(signal, 16)
            eng.dma_start(tile[full:full + 1, 0:rest], flat[full * EPP:count].unsqueeze(0)).then_inc(signal, 16)

        with nc.Block() as block:
            @block.gpsimd
            def _(pool):
                nc.gpsimd.memset(next_i[96:P], PAD_DST)
                nc.gpsimd.memset(attr[96:P], 0.0).then_inc(s_pads2, 1)
                pool.wait_ge(s_pads2, 1)
                nc.gpsimd.iota(digit_of, [[1, LO], [0, HCH]], base=0, channel_multiplier=0,
                               allow_small_or_imprecise_dtypes=True)
                nc.gpsimd.iota(lane_of, [[1, P], [0, TILES]], base=0, channel_multiplier=0,
                               allow_small_or_imprecise_dtypes=True)
                nc.gpsimd.iota(node_of, [[WIN, UN], [0, WT], [1, WIN]], base=0, channel_multiplier=0,
                               allow_small_or_imprecise_dtypes=True)
                nc.gpsimd.iota(iota_row[:, :], [[1, CH]], base=0, channel_multiplier=0,
                               allow_small_or_imprecise_dtypes=True)
                nc.gpsimd.iota(lanes, [[0, 1]], base=0, channel_multiplier=1, allow_small_or_imprecise_dtypes=True)
                nc.gpsimd.iota(steps5, [[WIN, 5]], base=0, channel_multiplier=0, allow_small_or_imprecise_dtypes=True)
                nc.gpsimd.iota(win_node[:, :], [[WIN, NW]], base=0, channel_multiplier=0,
                               allow_small_or_imprecise_dtypes=True)
                nc.gpsimd.iota(win_key[:, :], [[WKEYS, NW]], base=0, channel_multiplier=0,
                               allow_small_or_imprecise_dtypes=True).then_inc(s_iota, 1)
                nc.gpsimd.memset(zeros16[:, :], 0.0)
                nc.gpsimd.memset(ident[:, :], 0.0).then_inc(s_ident0, 1)
                pool.wait_ge(s_ident0, 1)
                nc.gpsimd.affine_select(out=ident[:, :], in_=ident[:, :], compare_op=ALU.not_equal, fill=1.0,
                                        base=0, pattern=[[-1, P]], channel_multiplier=1).then_inc(s_ident, 1)

            @block.sync
            def _(sp):
                sp.wait_ge(s_pads, 1)
                edges_in(sp, src_i, src, E, s_src)
                edges_in(sp, dst_i, dst, E, s_dst)
                sp.wait_ge(s_pads2, 1)
                edges_in(sp, next_i, dst[1:E], E - 1, s_next)
                sp.dma_start(attr[0:ROWS], edge_attr[0:ROWS * EPP, :].rearrange("(p e) k -> p e k", e=EPP)
                             ).then_inc(s_attr, 16)
                sp.dma_start(attr[ROWS:ROWS + 1, 0:REST], edge_attr[ROWS * EPP:E, :].unsqueeze(0)).then_inc(s_attr, 16)
                sp.wait_ge(s_codes, 1)
                sp.dma_start(src_lo_dram.rearrange("(p e) -> p e", e=EPP), src_lo).then_inc(s_codes_out, 16)
                sp.dma_start(src_hi_dram.rearrange("(p e) -> p e", e=EPP), src_hi).then_inc(s_codes_out, 16)
                sp.wait_ge(s_codes_out, 32)
                for g in range(GRP):
                    sp.dma_start(lo_bc[g * LO:(g + 1) * LO],
                                 src_lo_dram[g * HALF:(g + 1) * HALF].partition_broadcast(LO)).then_inc(s_bc, 16)
                    sp.dma_start(hi_bc[g * HI:(g + 1) * HI],
                                 src_hi_dram[g * HALF:(g + 1) * HALF].partition_broadcast(HI)).then_inc(s_bc, 16)
                sp.wait_ge(s_starts, 1)
                sp.dma_start(starts_dram.rearrange("(h q) -> q h", q=WQ), starts_i[0:WQ]).then_inc(s_starts_out, 16)
                sp.wait_ge(s_rowf, 1)
                sp.dma_start(dst_factor_dram.rearrange("(h l) -> l h", l=LO), t3[0:LO]).then_inc(s_rowf_out, 16)
                sp.wait_ge(s_starts_out, 16)
                sp.dma_start(starts_row[:, :], starts_dram.unsqueeze(0)).then_inc(s_starts_in, 16)
                sp.wait_ge(s_table, 1)
                sp.dma_start(edge_table.rearrange("(p e) w -> p (e w)", e=EPP),
                             table_tile.rearrange("p e w -> p (e w)")).then_inc(s_table_out, 16)
                sp.wait_ge(s_starts_in, 16)
                sp.wait_ge(s_rowf_out, 16)
                sp.wait_ge(s_table_out, 16)

            @block.vector
            def _(dve):
                steps = [0]

                def link(ins):
                    steps[0] += 1
                    ins.then_inc(s_dve1, 1)
                    dve.wait_ge(s_dve1, steps[0])

                nc.vector.memset(src_i[96:P], 0)
                nc.vector.memset(dst_i[96:P], PAD_DST).then_inc(s_pads, 1)
                nc.vector.memset(table_tile[:, :, 3:4], 0.0)
                dve.wait_ge(s_src, 32)
                link(nc.vector.tensor_scalar(tmp_i, src_i, LO - 1, None, ALU.bitwise_and))
                link(nc.vector.tensor_copy(src_lo, tmp_i))
                link(nc.vector.tensor_scalar(tmp_i, src_i, 6, None, ALU.logical_shift_right))
                nc.vector.tensor_copy(src_hi, tmp_i).then_inc(s_codes, 1)
                dve.wait_ge(s_codes, 1)
                dve.wait_ge(s_dst, 32)
                link(nc.vector.tensor_scalar(tmp_i, dst_i, LO - 1, None, ALU.bitwise_and))
                link(nc.vector.tensor_copy(dst_lo, tmp_i))
                link(nc.vector.tensor_scalar(tmp_i, dst_i, 6, None, ALU.logical_shift_right))
                link(nc.vector.tensor_copy(dst_hi, tmp_i))
                dve.wait_ge(s_iota, 1)

                def hist(t0, b):
                    for oh, digit, size in ((oh_lo, dst_lo, LO), (oh_hi, dst_hi, HI)):
                        last = nc.vector.tensor_tensor(oh[:, b], digit_of[:, 0:size], digit[:, bass.ds(t0, HCH)]
                                                       .unsqueeze(1).broadcast_to([P, size, HCH]), ALU.is_equal)
                    last.then_inc(s_hist_oh, 1)
                for b in range(2):
                    hist(b * HCH, b)
                with dve.Fori(1, HSTEPS // 2) as k:
                    for b in range(2):
                        dve.wait_ge(s_hist_mm, 2 * k + b - 1)
                        hist((2 * k + b) * HCH, b)
                link(nc.vector.tensor_copy(src_f, src_i))
                link(nc.vector.tensor_copy(dst_f, dst_i))
                link(nc.vector.tensor_scalar(tmp_i, src_i, P - 1, None, ALU.bitwise_and))
                link(nc.vector.tensor_copy(table_tile[:, :, 1], tmp_i))
                link(nc.vector.tensor_scalar(tmp_i, src_i, 7, None, ALU.logical_shift_right))
                nc.vector.scalar_tensor_tensor(table_tile[:, :, 0], dst_f, float(BLOCKS), tmp_i, ALU.mult, ALU.add)
                nc.vector.tensor_copy(table_tile[:, :, 2], dst_f)
                dve.wait_ge(s_next, 32)
                link(nc.vector.tensor_tensor(disorder, dst_i, next_i, ALU.is_gt))
                link(nc.vector.reduce_sum(bad, disorder, AX.X))
                nc.vector.memset(ones_t, 1.0)
                nc.vector.memset(ones1, 1.0)
                nc.vector.memset(dblk, 0.0)
                nc.vector.memset(dcol[:, :], 0.0)
                link(nc.vector.tensor_scalar(group_of[:, 1:2], lanes, float(HI), None, ALU.is_ge))
                nc.vector.tensor_scalar(group_of[:, 0:1], group_of[:, 1:2], -1.0, 1.0, ALU.mult, ALU.add)
                link(nc.vector.scalar_tensor_tensor(lane_hi, group_of[:, 1:2], -float(HI), lanes, ALU.mult, ALU.add))
                link(nc.vector.tensor_scalar(lane_lo, lanes, float(LO), None, ALU.is_ge))
                link(nc.vector.scalar_tensor_tensor(lane_lo, lane_lo, -float(LO), lanes, ALU.mult, ALU.add))
                link(nc.vector.tensor_scalar(below[0:LO], steps5[0:LO], lane_lo[0:LO], None, ALU.is_gt))
                link(nc.vector.tensor_tensor(within[0:LO], below[0:LO, 1:5], below[0:LO, 0:4], ALU.subtract))
                dve.wait_ge(s_ident, 1)
                nc.vector.tensor_copy(twice[0:LO, 0:LO], ident[0:LO, 0:LO])
                link(nc.vector.tensor_copy(twice[0:LO, LO:P], ident[0:LO, 0:LO]))
                dve.wait_ge(s_hist, 1)
                nc.vector.tensor_copy(t3[0:LO], banks[0][0:LO, 0:HI]).then_inc(s_deg, 1)
                dve.wait_ge(s_rep, 1)
                link(nc.vector.tensor_copy(deg, banks[1][:, 0:HI]))
                link(nc.vector.tensor_tensor_scan(t1[0:WQ], ones_t[0:WQ], banks[2][0:WQ, 0:HI], 0.0, ALU.mult, ALU.add))
                link(nc.vector.tensor_tensor(t1[0:WQ], t1[0:WQ], banks[2][0:WQ, 0:HI], ALU.subtract))
                link(nc.vector.tensor_tensor(t1[0:WQ], t1[0:WQ], banks[3][0:WQ, 0:HI], ALU.add))
                nc.vector.tensor_copy(starts_i[0:WQ], t1[0:WQ]).then_inc(s_starts, 1)
                link(nc.vector.tensor_scalar(t2[0:WQ], banks[4][0:WQ, 0:HI], float(CAP), None, ALU.is_gt))
                link(nc.vector.reduce_sum(bad4[0:WQ], t2[0:WQ], AX.X))
                link(nc.vector.tensor_tensor(bad[0:WQ], bad[0:WQ], bad4[0:WQ], ALU.add))
                nc.vector.tensor_copy(bad, bad).then_inc(s_bad, 1)
                nc.vector.tensor_scalar(t1, deg, 1.0, None, ALU.max).then_inc(s_clamped, 1)
                dve.wait_ge(s_clamped, 1)
                dve.wait_ge(s_sqrt, 1)
                link(nc.vector.reciprocal(dinv, t2))
                link(nc.vector.tensor_tensor(t3, dinv, dinv, ALU.mult))
                link(nc.vector.tensor_tensor(t3, t3, t1, ALU.mult))
                link(nc.vector.tensor_scalar(t3, t3, -0.5, 1.5, ALU.mult, ALU.add))
                link(nc.vector.tensor_tensor(dinv, dinv, t3, ALU.mult))
                link(nc.vector.tensor_scalar(t3, deg, 0.0, None, ALU.is_gt))
                link(nc.vector.tensor_tensor(dinv, dinv, t3, ALU.mult))
                nc.vector.tensor_scalar(t3, dinv, 1.0 / HSCALE, None, ALU.mult).then_inc(s_rowf, 1)
                nc.vector.tensor_scalar(dcol[0:LO, 0:BLOCKS], dinv[0:LO, 0:HI:2], HSCALE, None, ALU.mult)
                nc.vector.tensor_scalar(dcol[LO:P, 0:BLOCKS - 1], dinv[LO:P, 1:HI:2], HSCALE, None, ALU.mult)
                link(nc.vector.tensor_scalar(t1, dinv, DSCALE, None, ALU.mult))
                for g in range(GRP):
                    r = slice(g * LO, (g + 1) * LO)
                    link(nc.vector.tensor_copy(dblk[r, 0, g * HI:(g + 1) * HI], t1[r]))
                    link(nc.vector.tensor_tensor(dblk[r, 1, g * HI:(g + 1) * HI], t1[r],
                                                 dblk[r, 0, g * HI:(g + 1) * HI], ALU.subtract))
                nc.vector.tensor_copy(t2, t1).then_inc(s_dblk, 1)
                dve.wait_ge(s_badsum, 1)
                nc.vector.tensor_copy(flag_row[:, :], banks[5][0:1, 0:1])
                dve.wait_ge(s_bc, 16 * 2 * GRP)
                with dve.Fori(0, 7) as k:
                    part = lo_bc[:, bass.ds(k * (HALF // 7), HALF // 7)]
                    nc.vector.tensor_scalar(part, part, lane_lo, None, ALU.is_equal).then_inc(s_match, 1)
                with dve.Fori(0, LSTEPS // LUN) as k:
                    for j in range(LUN):
                        n = k * LUN + j
                        dve.wait_ge(s_look, n + 1)
                        dve.wait_ge(s_reduced, n + 1)
                        nc.vector.scalar_tensor_tensor(
                            picked[0:GRP * HI, j % LDEEP].rearrange("p t v -> p v t"),
                            hi_bc3[0:GRP * HI, :, bass.ds(n * LT, LT)], lane_hi[0:GRP * HI],
                            look_banks[j % LDEEP][0:GRP * HI, 0:LC].rearrange("p (v t) -> p v t", t=LT),
                            ALU.is_equal, ALU.mult).then_inc(s_picked, 1)
                dve.wait_ge(s_reduced, LSTEPS + LDEEP)
                for odd in range(2):
                    for g in range(GRP):
                        last = nc.vector.tensor_copy(src_factor[g * LO:(g + 1) * LO, odd:EPP:2],
                                                     banks[2][odd * LO:(odd + 1) * LO, g:EPP:2])
                link(last)
                dve.wait_ge(s_attr, 32)
                link(nc.vector.tensor_tensor(attr, attr, src_factor.unsqueeze(2).broadcast_to([P, EPP, K_ATTR]), ALU.mult))
                link(nc.vector.tensor_copy(attr16[:, :, 0:K_ATTR], attr))
                link(nc.vector.tensor_tensor(attr16[:, :, K_ATTR:2 * K_ATTR], attr, attr16[:, :, 0:K_ATTR], ALU.subtract))
                nc.vector.tensor_copy(table_tile[:, :, 4:8], attr16.bitcast(f32)).then_inc(s_table, 1)

            @block.scalar
            def _(act):
                act.wait_ge(s_clamped, 1)
                nc.scalar.activation(t2, t1, ACT.Sqrt).then_inc(s_sqrt, 1)

            @block.tensor
            def _(pe):
                pe.wait_ge(s_ident, 1)
                nc.tensor.matmul(banks[0][0:LO, 0:HI], zeros16[:, 0:LO], zeros16[:, 0:HI], start=True, stop=False)
                with pe.Fori(0, HSTEPS // 2) as k:
                    for b in range(2):
                        pe.wait_ge(s_hist_oh, 2 * k + b + 1)
                        for t in range(HCH):
                            last = nc.tensor.matmul(banks[0][0:LO, 0:HI], oh_lo[:, b, :, t], oh_hi[:, b, :, t],
                                                    start=False, stop=False)
                        last.then_inc(s_hist_mm, 1)
                nc.tensor.matmul(banks[0][0:LO, 0:HI], zeros16[:, 0:LO], zeros16[:, 0:HI], start=False,
                                 stop=True).then_inc(s_hist, 1)
                pe.wait_ge(s_deg, 1)
                nc.tensor.matmul(banks[1][:, 0:HI], twice[0:LO, :], t3[0:LO], start=True, stop=True)
                nc.tensor.matmul(banks[2][0:WQ, 0:HI], below[0:LO, 4:5].broadcast_to([LO, WQ]), t3[0:LO], start=True, stop=True)
                nc.tensor.matmul(banks[3][0:WQ, 0:HI], below[0:LO, 0:WQ], t3[0:LO], start=True, stop=True)
                nc.tensor.matmul(banks[4][0:WQ, 0:HI], within[0:LO], t3[0:LO], start=True, stop=True).then_inc(s_rep, 1)
                pe.wait_ge(s_bad, 1)
                nc.tensor.matmul(banks[5][0:1, 0:1], bad, ones1, start=True, stop=True).then_inc(s_badsum, 1)
                pe.wait_ge(s_dblk, 1)
                pe.wait_ge(s_match, 7)
                pe.sem_inc(s_reduced, LDEEP)

                def look(n, j):
                    for s in range(2):
                        last = nc.tensor.matmul(look_banks[j % LDEEP][0:GRP * HI, 0:LC], dblk[:, s, 0:GRP * HI],
                                                lo_bc3[:, :, bass.ds(n * LT, LT)], start=(s == 0), stop=(s == 1))
                    last.then_inc(s_look, 1)

                def reduce(n, j):
                    pe.wait_ge(s_picked, n + 1)
                    for m in range(LT // 2):
                        last = nc.tensor.matmul(banks[2][:, bass.ds((n * (LT // 2) + m) * GRP, GRP)],
                                                picked[0:GRP * HI, j % LDEEP, 2 * m:2 * m + 2, :].rearrange("p t v -> p (t v)"),
                                                group_of[0:GRP * HI], start=True, stop=True)
                    last.then_inc(s_reduced, 1)

                for j in range(LDEEP - 1):
                    look(j, j)

                def turn(k, last):
                    for j in range(LUN):
                        if not last or j + LDEEP - 1 < LUN:
                            look(k * LUN + j + LDEEP - 1, j + LDEEP - 1)
                        reduce(k * LUN + j, j)
                with pe.Fori(0, LSTEPS // LUN - 1) as k:
                    turn(k, False)
                turn(LSTEPS // LUN - 1, True)

        s_edges = [[sem(f"s_edges{h}{j}") for j in range(UN)] for h in range(2)]
        s_onehots, s_window, s_taken, s_keys = sem("s_onehots"), sem("s_window"), sem("s_taken"), sem("s_keys")
        s_all_oh, s_all_mm, s_all_block, s_all_taken = (sem(n) for n in ("s_all_oh", "s_all_mm", "s_all_block", "s_all_taken"))
        s_sums, s_part, s_parts_in, s_x = sem("s_sums"), sem("s_part"), sem("s_parts_in"), sem("s_x")

        def x_in(eng, tiles, signal):
            eng.dma_start(tiles[:, 0:BLOCKS - 1], x[0:(BLOCKS - 1) * P, :].rearrange("(i p) f -> p i f", p=P)).then_inc(signal, 16)
            eng.dma_start(tiles[0:TAIL, BLOCKS - 1], x[(BLOCKS - 1) * P:N, :]).then_inc(signal, 16)

        with nc.Block() as block:
            @block.sync
            def _(sp):
                irregular = sp.value_load(flag_row[0:1, 0:1])
                with sp.If(irregular > 0):
                    sp.wait_ge(s_sums, 1)
                    x_in(sp, x_tiles, s_x)
                with sp.Else():
                    x_in(sp, x_tiles, s_x)
                    def fetch(k, half, first):
                        _, starts = nc.values_load_multi_w_load_instructions(
                            starts_row[0:1, bass.ds(UN * k, UN)], engines=[sp.engine], min_val=0, max_val=E,
                            skip_runtime_bounds_check_because="a start is a count of some of the E edges")
                        for j, start in enumerate(starts):
                            w = UN * k + j
                            if not first:
                                sp.wait_ge(s_window, w - 2 * UN + 1)
                            sp.dma_start(edge_buf[:, half, j].rearrange("p k w -> p (k w)"),
                                         edge_table[bass.ds(start, CAP), :].rearrange("(p k) w -> p (k w)", k=WT)
                                         ).then_inc(s_edges[half][j], 16)
                    fetch(0, 0, True)
                    fetch(1, 1, True)
                    with sp.Fori(1, NW // UN // 2) as k:
                        fetch(2 * k, 0, False)
                        fetch(2 * k + 1, 1, False)
                    fetch(NW // UN - 1, 0, False)
                sp.wait_ge(s_part, 2)
                for s in range(2):
                    r = LO + K_ATTR * s
                    sp.dma_start(counts3[r:r + K_ATTR, BLOCKS - 1, :], attr_parts[:, s, :]).then_inc(s_parts_in, 16)
                sp.wait_ge(s_parts_in, 32)

            @block.vector
            def _(dve):
                irregular = dve.value_load(flag_row[0:1, 0:1])
                with dve.If(irregular > 0):
                    def all_edges(first, t, node0):
                        dve.wait_ge(s_all_mm, first)
                        for c in range(NCH):
                            last = nc.vector.tensor_scalar(all_dst[:, c * CH:(c + 1) * CH], iota_row[:, :], float(c * CH),
                                                           dst_f[:, bass.ds(t, 1)], ALU.add, ALU.is_equal)
                        if node0 is not None:
                            last = nc.vector.tensor_scalar(all_src, iota_row[:, 0:P], node0,
                                                           src_f[:, bass.ds(t, 1)], ALU.add, ALU.is_equal)
                        last.then_inc(s_all_oh, 1)
                    with dve.Fori(0, BLOCKS) as a:
                        with dve.Fori(0, EPP) as t:
                            all_edges(a * EPP + t + 1, t, win_node[:, bass.ds(a * (P // WIN), 1)])
                    with dve.Fori(0, EPP) as t:
                        all_edges(BLOCKS * EPP + t + 1, t, None)
                with dve.Else():
                    def onehots(k, b, turn, first):
                        flat = edge_buf[:, b].rearrange("p j t w -> p (j t) w")
                        if not first:
                            dve.wait_ge(s_window, UN * (k - 1))
                        for j in range(UN):
                            dve.wait_ge(s_edges[b][j], 16 * turn + 16)
                        nc.vector.tensor_tensor(own_key[:, b].rearrange("p (j t) -> p j t", j=UN), edge_buf[:, b, :, :, 0],
                                                win_key[:, bass.ds(UN * k, UN)].unsqueeze(2).broadcast_to([P, UN, WT]),
                                                ALU.subtract)
                        nc.vector.tensor_copy(lane16[:, b], flat[:, :, 1]).then_inc(s_keys, 1)
                        nc.vector.scalar_tensor_tensor(oh_dst[:, b], flat[:, :, 2:3].broadcast_to([P, TILES, WIN]),
                                                       win_node[:, bass.ds(UN * k, 1)],
                                                       node_of.rearrange("p (n v) -> p n v", v=WIN),
                                                       ALU.subtract, ALU.is_equal)
                        dve.wait_ge(s_keys, k + 1)
                        nc.vector.tensor_tensor(oh_src[:, b], lane_of,
                                                lane16[:, b].unsqueeze(1).broadcast_to([P, P, TILES]), ALU.is_equal)
                        for j in range(UN):
                            if not (first and b == 0):
                                dve.wait_ge(s_window, UN * k + j - UN + 1)
                            for t in range(WT):
                                n = WT * j + t
                                last = nc.vector.tensor_scalar(oh_key[:, j, t, :], iota_row[:, 0:WKEYS],
                                                               own_key[:, b, n:n + 1], None, ALU.is_equal)
                            last.then_inc(s_onehots, 1)
                    onehots(0, 0, 0, True)
                    onehots(1, 1, 0, True)
                    with dve.Fori(1, NW // UN // 2) as k:
                        onehots(2 * k, 0, k, False)
                        onehots(2 * k + 1, 1, k, False)
                    onehots(NW // UN - 1, 0, NW // UN // 2, False)
                dve.wait_ge(s_sums, 1)
                nc.vector.tensor_copy(attr_parts[:, 0, :], attr_sums).then_inc(s_part, 1)
                dve.wait_ge(s_part, 1)
                nc.vector.tensor_tensor(attr_parts[:, 1, :], attr_sums, attr_parts[:, 0, :], ALU.subtract).then_inc(s_part, 1)

            @block.tensor
            def _(pe):
                irregular = pe.value_load(flag_row[0:1, 0:1])
                with pe.If(irregular > 0):
                    def all_edges(base, lhsT, rows):
                        for c in range(NCH):
                            nc.tensor.matmul(banks[c][0:rows, 0:CH], zeros16[:, 0:rows], zeros16[:, :], start=True, stop=False)
                        with pe.Fori(0, EPP) as t:
                            pe.wait_ge(s_all_oh, base + t + 1)
                            parts = lhsT(t)
                            for w in parts:
                                for c in range(NCH):
                                    last = nc.tensor.matmul(banks[c][0:rows, 0:CH], w, all_dst[:, c * CH:(c + 1) * CH],
                                                            start=False, stop=False)
                            last.then_inc(s_all_mm, 1)
                        for c in range(NCH):
                            last = nc.tensor.matmul(banks[c][0:rows, 0:CH], zeros16[:, 0:rows], zeros16[:, :], start=False, stop=True)
                        last.then_inc(s_all_block, 1)
                    pe.sem_inc(s_all_mm, 1)
                    with pe.Fori(0, BLOCKS) as a:
                        pe.wait_ge(s_all_taken, a + 1)
                        all_edges(a * EPP, lambda t: [all_src], P)
                    pe.wait_ge(s_all_taken, BLOCKS + 1)
                    all_edges(BLOCKS * EPP, lambda t: [attr16[:, bass.ds(t, 1), K_ATTR * s:K_ATTR * (s + 1)]
                                                       .rearrange("p o k -> p (o k)") for s in range(2)], K_ATTR)
                with pe.Else():
                    def products(k, half, first):
                        for j in range(UN):
                            w = UN * k + j
                            b = j % 2
                            pe.wait_ge(s_onehots, w + 1)
                            if not (first and j < 2):
                                pe.wait_ge(s_taken, w - 1)
                            for t in range(WT):
                                n = WT * j + t
                                nc.tensor.matmul(banks[b][:, 0:WKEYS], oh_src[:, half, :, n], oh_key[:, j, t, :],
                                                 start=(t == 0), stop=(t == WT - 1))
                            for t in range(WT):
                                n = WT * j + t
                                a16 = edge_buf[:, half, j, t, 4:8].bitcast(f16)
                                for s in range(2):
                                    last = nc.tensor.matmul(banks[2 + b][0:K_ATTR, 0:WIN], a16[:, K_ATTR * s:K_ATTR * (s + 1)],
                                                            oh_dst[:, half, n, :], start=(t == 0 and s == 0),
                                                            stop=(t == WT - 1 and s == 1))
                            last.then_inc(s_window, 1)
                    products(0, 0, True)
                    products(1, 1, False)
                    with pe.Fori(1, NW // UN // 2) as k:
                        products(2 * k, 0, False)
                        products(2 * k + 1, 1, False)
                    products(NW // UN - 1, 0, False)

            @block.scalar
            def _(act):
                irregular = act.value_load(flag_row[0:1, 0:1])
                with act.If(irregular > 0):
                    act.sem_inc(s_all_taken, 1)
                    with act.Fori(0, BLOCKS) as a:
                        act.wait_ge(s_all_block, a + 1)
                        for c in range(NCH):
                            last = nc.scalar.copy(countsT[:, bass.ds(a * NP + c * CH, CH)], banks[c][:, 0:CH])
                        last.then_inc(s_all_taken, 1)
                    act.wait_ge(s_all_block, BLOCKS + 1)
                    for c in range(NCH):
                        last = nc.scalar.mul(attr_sums[:, c * CH:(c + 1) * CH], banks[c][0:K_ATTR, 0:CH], 1.0 / DSCALE)
                    last.then_inc(s_sums, 1)
                with act.Else():
                    with act.Fori(0, NW // UN) as k:
                        for j in range(UN):
                            w = UN * k + j
                            act.wait_ge(s_window, w + 1)
                            nc.scalar.copy(counts3[:, :, bass.ds(w * WIN, WIN)],
                                           banks[j % 2][:, 0:WKEYS].rearrange("p (d a) -> p a d", a=BLOCKS))
                            nc.scalar.mul(attr_sums[:, bass.ds(w * WIN, WIN)], banks[2 + j % 2][0:K_ATTR, 0:WIN],
                                          1.0 / DSCALE).then_inc(s_taken, 1)
                    act.wait_ge(s_taken, NW)
                    act.sem_inc(s_sums, 1)

        s_aff, s_h, s_lnz = sem("s_aff"), sem("s_h"), sem("s_lnz")
        s_chain, s_var, s_root, s_ln, s_h0 = (sem(n) for n in ("s_chain", "s_var", "s_root", "s_ln", "s_h0"))
        s_h0T, s_norm, s_tr, s_hi, s_parts = (sem(n) for n in ("s_h0T", "s_norm", "s_tr", "s_hi", "s_parts"))
        s_ew, s_ewhi, s_ewparts, s_w, s_df = (sem(n) for n in ("s_ew", "s_ewhi", "s_ewparts", "s_w", "s_df"))
        s_sum = [sem("s_sum0"), sem("s_sum1")]
        s_agg = [sem("s_agg0"), sem("s_agg1")]
        s_mlp, s_relu, s_bnvar, s_bnroot, s_affine = (sem(n) for n in ("s_mlp", "s_relu", "s_bnvar", "s_bnroot", "s_affine"))
        s_xr, s_res, s_out = sem("s_xr"), sem("s_res"), sem("s_out")

        mean_var = mv_a[:, :].rearrange("p (i v) -> p i v", v=2)
        ln_v, ln_r, ln_t, ln_b = (mv[:, BLOCKS * n:BLOCKS * (n + 1)] for n in range(4))
        stats4 = stats[:, :].rearrange("p (f c s) -> p f c s", f=HALVES, s=6)
        ln_stats = work[:, 0:6 * BLOCKS].rearrange("p (i s) -> p i s", s=6)
        bn_mv = small[:, 0:4].rearrange("p (f v) -> p f v", f=HALVES)
        bn_v, bn_r, bn_t, bn_scale, bn_shift = (small[:, 4 + 2 * n:6 + 2 * n] for n in range(5))
        EWR = slice(LO, LO + 2 * K_ATTR)
        x_again = countsT[:, 0:2 * BLOCKS * D].bitcast(f32).rearrange("p (i f) -> p i f", i=BLOCKS)
        out_tiles = countsT[:, 2 * BLOCKS * D:4 * BLOCKS * D].bitcast(f32).rearrange("p (i f) -> p i f", i=BLOCKS)

        def nodes(i):
            return P if i < BLOCKS - 1 else TAIL

        with nc.Block() as block:
            @block.sync
            def _(sp):
                for n, v in enumerate((mlp_b, bn_g, bn_b)):
                    sp.dma_start(aff[:, n, :], v.rearrange("l (f p) -> p (l f)", p=P)).then_inc(s_aff, 16)
                sp.wait_ge(s_lnz, 1)

                def layer(l):
                    sp.wait_ge(s_mlp, l * NCH + 1)
                    sp.dma_start(weights, mlp_w[bass.ds(l, 1)].rearrange("l (k p) n -> p (l k) n", p=P)).then_inc(s_w, 16)
                    sp.wait_ge(s_ewparts, l + 1)
                    for s in range(2):
                        r = LO + K_ATTR * s
                        sp.dma_start(ewt[r:r + 3, P:D], ew2[bass.ds(l, 1)].rearrange("l k n -> (l k) n")).then_inc(s_ew, 16)
                        sp.dma_start(ewt[r + 3:r + 4, 0:P], ew1[bass.ds(l, 1)].rearrange("l k n -> (l k) n")).then_inc(s_ew, 16)
                    with sp.Fori(0, NCH) as c:
                        sp.wait_ge(s_agg[1], l * NCH + c + 1)
                        sp.dma_start(dst_factor, dst_factor_dram[bass.ds(c * CH, CH)].partition_broadcast(P)).then_inc(s_df, 16)
                with sp.Fori(0, L) as l:
                    layer(l)
                sp.wait_ge(s_mlp, L * NCH + 1)
                x_in(sp, x_again, s_xr)
                for g in range(NBQ):
                    i0, i1 = g * BQ, (g + 1) * BQ
                    sp.wait_ge(s_res, i1)
                    if i1 == BLOCKS:
                        i1 -= 1
                        sp.dma_start(out[i1 * P:N, :], out_tiles[0:TAIL, i1]).then_inc(s_out, 16)
                    sp.dma_start(out[i0 * P:i1 * P, :].rearrange("(i p) f -> p i f", p=P), out_tiles[:, i0:i1]).then_inc(s_out, 16)
                sp.wait_ge(s_out, 16 * (NBQ + 1))

            @block.gpsimd
            def _(pool):
                nc.gpsimd.memset(ewt[:, :], 0.0).then_inc(s_ewparts, 1)

            @block.vector
            def _(dve):
                steps = [0]

                def link(ins):
                    steps[0] += 1
                    ins.then_inc(s_chain, 1)
                    dve.wait_ge(s_chain, steps[0])

                def newton(v, r, t, chain):
                    chain(nc.vector.reciprocal(r, r))
                    chain(nc.vector.tensor_tensor(t, r, r, ALU.mult))
                    chain(nc.vector.tensor_tensor(t, t, v, ALU.mult))
                    chain(nc.vector.tensor_scalar(t, t, -0.5, 1.5, ALU.mult, ALU.add))
                    chain(nc.vector.tensor_tensor(r, r, t, ALU.mult))

                link(nc.vector.memset(mv_a[:, :], 0.0))
                dve.wait_ge(s_x, 32)
                for i in range(BLOCKS):
                    last = nc.vector.bn_stats(ln_stats[0:nodes(i), i], x_tiles[0:nodes(i), i])
                link(last)
                for i in range(BLOCKS):
                    last = nc.vector.bn_aggr(mean_var[0:nodes(i), i], ln_stats[0:nodes(i), i])
                link(last)
                dve.sem_inc(s_lnz, 1)
                nc.vector.tensor_scalar(ln_v, mean_var[:, :, 1], EPS, None, ALU.add).then_inc(s_var, 1)
                dve.wait_ge(s_var, 1)
                dve.wait_ge(s_root, 1)
                newton(ln_v, ln_r, ln_t, link)
                nc.vector.scalar_tensor_tensor(ln_b, mean_var[:, :, 0], -1.0, ln_r, ALU.mult, ALU.mult).then_inc(s_ln, 1)
                nc.vector.memset(hT3[:, :, N:NP], 0.0)
                for i in range(BLOCKS):
                    dve.wait_ge(s_h0T, i + 1)
                    last = nc.vector.tensor_copy(hT3[:, :, i * P:i * P + nodes(i)],
                                                 banks[4 + i % 2][:, 0:D].rearrange("p (f n) -> p f n", f=HALVES)[:, :, 0:nodes(i)])
                    last.then_inc(s_h0, 1)
                dve.wait_ge(s_h0, BLOCKS)
                dve.sem_inc(s_norm, NBQ)
                nc.vector.memset(hs4[:, BLOCKS - 1], 0.0).then_inc(s_lnz, 1)
                for h in range(2):
                    dve.sem_inc(s_agg[h], 1)
                base = steps[0]
                CHAIN = 11

                def layer(l):
                    dve.wait_ge(s_ewhi, l + 1)
                    nc.vector.scalar_tensor_tensor(hs4[EWR, BLOCKS - 1, 1], ewt[EWR, :], HSCALE, hs4[EWR, BLOCKS - 1, 0],
                                                   ALU.mult, ALU.subtract).then_inc(s_ewparts, 1)
                    for i in range(BLOCKS):
                        dve.wait_ge(s_hi, l * BLOCKS + i + 1)
                        n = nodes(i)
                        nc.vector.scalar_tensor_tensor(hs4[0:n, i, 1], banks[4 + i % 2][0:n, 0:D], dcol[0:n, i:i + 1],
                                                       hs4[0:n, i, 0], ALU.mult, ALU.subtract).then_inc(s_parts, 1)

                    def take(n, h):
                        dve.wait_ge(s_sum[h], n + 1)
                        dve.wait_ge(s_mlp, n + 1)
                        if h == 0:
                            dve.wait_ge(s_df, 16 * n + 16)
                        nc.vector.tensor_tensor(agg[:, h, :], banks[h][:, 0:CH], dst_factor, ALU.mult).then_inc(s_agg[h], 1)

                    def chunk_stats(n, c, size):
                        dve.wait_ge(s_relu, n + 2)
                        for f in range(HALVES):
                            last = nc.vector.bn_stats(stats4[:, f, c, :] if isinstance(c, int) else
                                                      stats4[:, f, bass.ds(c, 1), :].rearrange("p c s -> p (c s)"),
                                                      hT3[:, f, bass.ds(c * CH, size)])
                        return last
                    take(l * NCH, 0)
                    take(l * NCH, 1)
                    with dve.Fori(1, NCH) as c:
                        take(l * NCH + c, 0)
                        chunk_stats(l * NCH + c - 1, c - 1, CH)
                        take(l * NCH + c, 1)
                    count = [0]

                    def chain(ins):
                        count[0] += 1
                        ins.then_inc(s_chain, 1)
                        dve.wait_ge(s_chain, l * CHAIN + base + count[0])
                    chain(chunk_stats(l * NCH + NCH - 1, NCH - 1, LAST_CH))
                    nc.vector.memset(bn_shift, 0.0)
                    for f in range(HALVES):
                        last = nc.vector.bn_aggr(bn_mv[:, f], stats4[:, f].rearrange("p c s -> p (c s)"))
                    chain(last)
                    chain(nc.vector.tensor_scalar(bn_v, bn_mv[:, :, 1], EPS, None, ALU.add))
                    nc.vector.tensor_copy(bn_t, bn_v).then_inc(s_bnvar, 1)
                    dve.wait_ge(s_bnroot, l + 1)
                    newton(bn_v, bn_r, bn_t, chain)
                    cols = bass.ds(l * HALVES, HALVES)
                    chain(nc.vector.tensor_tensor(bn_scale, bn_r, aff[:, 1, cols], ALU.mult))
                    chain(nc.vector.tensor_tensor(bn_t, bn_mv[:, :, 0], bn_scale, ALU.mult))
                    chain(nc.vector.tensor_tensor(bn_shift, aff[:, 2, cols], bn_t, ALU.subtract))
                    assert count[0] == CHAIN, count
                    dve.sem_inc(s_affine, 1)

                dve.wait_ge(s_aff, 48)
                with dve.Fori(0, L) as l:
                    layer(l)
                dve.wait_ge(s_xr, 32)
                for i in range(BLOCKS):
                    n = nodes(i)
                    dve.wait_ge(s_tr, L * BLOCKS + i + 1)
                    nc.vector.tensor_tensor(out_tiles[0:n, i], banks[4 + i % 2][0:n, 0:D], x_again[0:n, i], ALU.add).then_inc(s_res, 1)

            @block.scalar
            def _(act):
                act.wait_ge(s_var, 1)
                nc.scalar.activation(ln_r, ln_v, ACT.Sqrt).then_inc(s_root, 1)
                act.wait_ge(s_ln, 1)
                for i in range(BLOCKS):
                    n = nodes(i)
                    nc.scalar.activation(x_tiles[0:n, i], x_tiles[0:n, i], ACT.Relu, bias=ln_b[0:n, i:i + 1],
                                         scale=ln_r[0:n, i:i + 1]).then_inc(s_h, 1)
                act.wait_ge(s_lnz, 2)
                act.sem_inc(s_relu, 1)

                def normalize(g, func):
                    cols = slice(g * BQ * P, min((g + 1) * BQ * P, NP))
                    for f in range(HALVES):
                        last = nc.scalar.activation(hT3[:, f, cols], hT3[:, f, cols], func, bias=bn_shift[:, f:f + 1],
                                                    scale=bn_scale[:, f:f + 1])
                    last.then_inc(s_norm, 1)

                def layer(l, first):
                    if not first:
                        normalize(0, ACT.Relu)
                    act.wait_ge(s_ew, 64 * l + 64)
                    nc.scalar.mul(hs4[EWR, BLOCKS - 1, 0], ewt[EWR, :], HSCALE).then_inc(s_ewhi, 1)
                    for i in range(BLOCKS):
                        if not first and i % BQ == 0 and i // BQ + 1 < NBQ:
                            normalize(i // BQ + 1, ACT.Relu)
                        n = nodes(i)
                        act.wait_ge(s_tr, l * BLOCKS + i + 1)
                        nc.scalar.activation(hs4[0:n, i, 0], banks[4 + i % 2][0:n, 0:D], ACT.Copy,
                                             scale=dcol[0:n, i:i + 1]).then_inc(s_hi, 1)
                    with act.Fori(0, NCH) as c:
                        act.wait_ge(s_mlp, l * NCH + c + 2)
                        for f in range(HALVES):
                            last = nc.scalar.activation(hT3[:, f, bass.ds(c * CH, CH)], banks[2 + f][:, 0:CH], ACT.Relu,
                                                        bias=aff[:, 0, bass.ds(l * HALVES + f, 1)])
                        last.then_inc(s_relu, 1)
                    act.wait_ge(s_bnvar, l + 1)
                    nc.scalar.activation(bn_r, bn_v, ACT.Sqrt).then_inc(s_bnroot, 1)
                    act.wait_ge(s_affine, l + 1)

                act.wait_ge(s_aff, 48)
                layer(0, True)
                with act.Fori(1, L) as l:
                    layer(l, False)
                for g in range(NBQ):
                    normalize(g, ACT.Identity)

            @block.tensor
            def _(pe):
                for i in range(BLOCKS):
                    n = nodes(i)
                    pe.wait_ge(s_h, i + 1)
                    if i >= 2:
                        pe.wait_ge(s_h0, i - 1)
                    for f in range(HALVES):
                        last = nc.tensor.transpose(banks[4 + i % 2][:, f * P:f * P + n], x_tiles[0:n, i, f * P:(f + 1) * P],
                                                   ident[0:n, 0:n])
                    last.then_inc(s_h0T, 1)
                pe.sem_inc(s_mlp, 1)

                def turned(l, i):
                    n = nodes(i)
                    if i % BQ == 0:
                        pe.wait_ge(s_norm, l * NBQ + i // BQ + 1)
                    for f in range(HALVES):
                        last = nc.tensor.transpose(banks[4 + i % 2][0:n, f * P:(f + 1) * P],
                                                   hT3[:, f, i * P:i * P + n], ident[:, :])
                    last.then_inc(s_tr, 1)

                def layer(l):
                    turned(l, 0)
                    turned(l, 1)
                    for i in range(BLOCKS):
                        pe.wait_ge(s_parts, l * BLOCKS + i + 1)
                        if i == BLOCKS - 1:
                            pe.wait_ge(s_ewparts, l + 2)
                        for h in range(2):
                            if i == 0:
                                pe.wait_ge(s_agg[h], l * NCH + 1)
                            for s in range(2):
                                last = nc.tensor.matmul(banks[h][:, 0:CH], hs4[:, i, s, h * P:(h + 1) * P],
                                                        countsT[:, i * NP:i * NP + CH],
                                                        start=(i == 0 and s == 0), stop=(i == BLOCKS - 1 and s == 1))
                            if i == BLOCKS - 1:
                                last.then_inc(s_sum[h], 1)
                            if h == 0 and i + 2 < BLOCKS:
                                turned(l, i + 2)

                    def sums(n, c, h):
                        pe.wait_ge(s_agg[h], n + 1)
                        for i in range(BLOCKS):
                            for s in range(2):
                                last = nc.tensor.matmul(banks[h][:, 0:CH], hs4[:, i, s, h * P:(h + 1) * P],
                                                        countsT[:, bass.ds(c * CH + i * NP, CH)],
                                                        start=(i == 0 and s == 0), stop=(i == BLOCKS - 1 and s == 1))
                        last.then_inc(s_sum[h], 1)

                    def mlp(n, c):
                        pe.wait_ge(s_w, 16 * l + 16)
                        for h in range(2):
                            pe.wait_ge(s_agg[h], n + 2)
                        pe.wait_ge(s_relu, n + 1)
                        for f in range(HALVES):
                            for k in range(4):
                                rhs = hT3[:, k, bass.ds(c * CH, CH)] if k < 2 else agg[:, k - 2, :]
                                last = nc.tensor.matmul(banks[2 + f][:, 0:CH], weights[:, k, f * P:(f + 1) * P], rhs,
                                                        start=(k == 0), stop=(k == 3))
                        last.then_inc(s_mlp, 1)

                    with pe.Fori(1, NCH) as c:
                        sums(l * NCH + c, c, 0)
                        mlp(l * NCH + c - 1, c - 1)
                        sums(l * NCH + c, c, 1)
                    mlp(l * NCH + NCH - 1, NCH - 1)

                with pe.Fori(0, L) as l:
                    layer(l)
                for i in range(BLOCKS):
                    if 2 <= i < BLOCKS - 1:
                        pe.wait_ge(s_res, i - 1 + (i == BLOCKS - 2))
                    turned(L, i)


_INS = ["x", "src", "dst", "edge_attr_4", "L0_gnn_mlp_w", "L0_gnn_mlp_b", "L0_gnn_ew1", "L0_gnn_ew2", "L0_gnn_bn_g", "L0_gnn_bn_b"]


def kernel(**inputs):
    import numpy as _np
    import concourse.bacc as _bacc
    from concourse import mybir as _mybir
    from concourse.bass_utils import run_bass_kernel_spmd as _run

    nc = _bacc.Bacc("TRN2", target_bir_lowering=False, num_devices=1, dynamic_dma_scratch_size=1024)
    arrays, args = {}, []
    for name in _INS:
        a = _np.ascontiguousarray(inputs[name])
        arrays[f"in_{name}"] = a
        args.append(nc.dram_tensor(f"in_{name}", a.shape, _mybir.dt.from_np(a.dtype), kind="ExternalInput").ap())
    shape = inputs["x"].shape
    args.append(nc.dram_tensor("out_0", shape, _mybir.dt.float32, kind="ExternalOutput").ap())
    gnn_program(nc, *args)
    r = _run(nc, [arrays], core_ids=[0])
    return r.results[0]["out_0"]
```

```python
import concourse.bass as bass
from concourse import mybir
from contextlib import ExitStack


def gnn_program(nc, x, src, dst, edge_attr, mlp_w, mlp_b, ew1, ew2, bn_g, bn_b, out):
    f32, f16, i32 = mybir.dt.float32, mybir.dt.float16, mybir.dt.int32
    ALU, ACT, AX = mybir.AluOpType, mybir.ActivationFunctionType, mybir.AxisListType

    P = 128
    N, D = x.shape
    E = src.shape[0]
    K_ATTR = edge_attr.shape[1]
    L = mlp_w.shape[0]
    HALVES = D // P
    BLOCKS = -(-N // P)
    TAIL = N - (BLOCKS - 1) * P
    LO, HI = 64, 49
    NP = LO * HI
    WIN = 18
    NW = -(-N // WIN)
    WKEYS = BLOCKS * WIN
    WT = 3
    CAP = WT * P
    UN = 6
    TURNS = NW // UN
    WDEEP = 3
    LRUN = 6
    TW_NODES = UN * WIN
    LNB = 2
    LN_TURNS = (BLOCKS - 1) // LNB
    LN_FIRST = 2
    CH = 512
    NCH = -(-NP // CH)
    LAST = NCH - 1
    TAIL_CH = NP - LAST * CH
    GCH = 448
    NG = NP // GCH
    CB = CH // P
    NPC = NCH + 1
    MB = 3
    TB = 4
    EPP = 420
    EP = P * EPP
    ROWS = E // EPP
    REST = E - ROWS * EPP
    PAD_DST = 4000
    LT = 20
    LDEEP = 3
    LSTEPS = EPP // LT
    LTURNS = LSTEPS // LDEEP
    TURN_EDGES = LDEEP * LT
    HCH = 42
    HSTEPS = EPP // HCH
    TW = 3 + 2 * K_ATTR
    DSCALE = 1024.0
    ZSCALE = 64.0
    HMUL = 16.0
    WMUL = 256.0
    NSCALE = 1.0 / 16
    EPS = 1e-5
    BQ = 5
    NBQ = BLOCKS // BQ
    assert NP >= N and NP % GCH == 0 and TAIL_CH <= LO and EP >= E + CAP and BLOCKS * P >= N and D == 2 * P
    assert LTURNS * LDEEP * LT == EPP and LT * BLOCKS <= 512 and EPP % HCH == 0 and HSTEPS % 2 == 0 and NW % UN == 0 and TURNS % 2 == 1 and UN % WDEEP == 0
    assert (PAD_DST * NSCALE) ** 2 < 65504 and PAD_DST >= NP and BLOCKS % BQ == 0 and TAIL <= LO and NW * WIN < NP and (BLOCKS - 1) % LNB == 0 and LN_FIRST + 2 * LN_TURNS <= TURNS

    ctx = ExitStack()
    with ctx:
        ctx.enter_context(nc.allow_non_contiguous_dma(reason="short tables, once"))

        def sb(name, shape, dt):
            return ctx.enter_context(nc.sbuf_tensor(name, shape, dt))

        def sem(name):
            return ctx.enter_context(nc.semaphore(name))

        edge_table = nc.dram_tensor("edge_table", [EP, TW], f32).ap()
        src_lane_dram = nc.dram_tensor("src_lane_dram", [EP], f16).ap()
        dst_factor_dram = nc.dram_tensor("dst_factor_dram", [NP], f32).ap()
        starts_dram = nc.dram_tensor("starts_dram", [NP], i32).ap()

        countsT = sb("countsT", [P, BLOCKS * NP], f16)
        hT = sb("hT", [P, HALVES * NP], f32)
        hs = sb("hs", [P, BLOCKS * 2 * D], f16)
        work = sb("work", [P, 3584], f32)
        hT3 = hT[:, :].rearrange("p (f n) -> p f n", f=HALVES)
        hs4 = hs[:, :].rearrange("p (i s f) -> p i s f", i=BLOCKS, s=2)
        counts3 = countsT[:, :].rearrange("p (a n) -> p a n", a=BLOCKS)

        iota_row = sb("iota_row", [P, max(GCH, WKEYS)], f16)
        zeros16 = sb("zeros16", [P, GCH], f16)
        ident = sb("ident", [P, P], f32)
        flag_row = sb("flag_row", [1, 1], i32)
        dcol = sb("dcol", [P, BLOCKS], f32)
        aff = sb("aff", [P, 3, L * HALVES], f32)
        ew_cols = sb("ew_cols", [P, L, HALVES, 2 * K_ATTR], f32)
        ew_now = sb("ew_now", [P, HALVES, 2 * K_ATTR], f32)
        stats = sb("stats", [P, HALVES * NCH * 6], f32)
        small = sb("small", [P, 24], f32)
        mv = sb("mv", [P, 4 * BLOCKS], f32)
        ln_sums = sb("ln_sums", [P, 3 * BLOCKS], f32)
        one = sb("one", [P, 1], f32)
        high_sign = sb("high_sign", [P, 1], f32)
        sum_scale = sb("sum_scale", [P, 1], f32)
        EWR = slice(LO, LO + 2 * K_ATTR)
        ln_sum, ln_square, ln_minus_mean = (ln_sums[:, n * BLOCKS:(n + 1) * BLOCKS] for n in range(3))

        def early(lo, n, dt=f16):
            view = countsT[:, lo:lo + n]
            return view if dt == f16 else view.bitcast(dt)
        lane_bc = early(0, EP)
        lane_bc3 = lane_bc.rearrange("p (m t) -> p m t", t=TURN_EDGES)
        oh_lo = early(EP, 2 * HCH * LO).rearrange("p (b v t) -> p b v t", b=2, v=LO)
        oh_hi = early(EP + 2 * HCH * LO, 2 * HCH * HI).rearrange("p (b v t) -> p b v t", b=2, v=HI)
        o = EP + 2 * HCH * (LO + HI)
        digit_of = early(o, HCH * LO).rearrange("p (v t) -> p v t", v=LO)
        o += HCH * LO
        block_of = early(o, BLOCKS * LT).rearrange("p (a t) -> p a t", a=BLOCKS)
        o += BLOCKS * LT
        table_tile = early(o, 2 * EPP * TW, f32).rearrange("p (e w) -> p e w", w=TW)
        assert o + 2 * EPP * TW <= BLOCKS * NP
        table_attr = early(o, 2 * EPP * TW).rearrange("p (e w) -> p e w", w=2 * TW)[:, :, 6:2 * TW].rearrange(
            "p e (v s k) -> p e v s k", v=2, s=2)
        picked = early(EP, LDEEP * 2 * LT * BLOCKS, f32).rearrange("p (b t a) -> p b t a", b=LDEEP, t=LT)
        o = EP + LDEEP * 2 * LT * BLOCKS
        oh_block = early(o, LDEEP * LT * BLOCKS).rearrange("p (b a t) -> p b a t", b=LDEEP, a=BLOCKS)
        assert LDEEP * 3 * LT * BLOCKS <= 2 * HCH * (LO + HI)

        hs_f = hs[:, :].bitcast(f32)
        src_f = hs_f[:, 0:EPP]
        dst_f = hs_f[:, EPP:2 * EPP]
        src_i = hs_f[:, 2 * EPP:3 * EPP].bitcast(i32)
        dst_i = hs_f[:, 3 * EPP:4 * EPP].bitcast(i32)
        tmp_i = hs_f[:, 4 * EPP:5 * EPP].bitcast(i32)
        next_i = hs_f[:, 5 * EPP:6 * EPP].bitcast(i32)
        attr16 = hs_f[:, 6 * EPP:14 * EPP].bitcast(f16).rearrange("p (e k) -> p e k", k=4 * K_ATTR)
        all_dst = hs_f[:, 2 * EPP:2 * EPP + NP // 2].bitcast(f16)
        all_src = hs_f[:, 2 * EPP + NP // 2:2 * EPP + NP // 2 + P // 2].bitcast(f16)
        all_attr = all_src[:, 0:4 * K_ATTR]
        assert 2 * EPP + NP // 2 + P // 2 <= 6 * EPP and 14 * EPP <= BLOCKS * D
        x_tiles = hs_f[:, 0:BLOCKS * D].rearrange("p (i f) -> p i f", i=BLOCKS)

        attr = hT[:, 0:EPP * K_ATTR].rearrange("p (e k) -> p e k", k=K_ATTR)
        q = EPP * K_ATTR
        src_factor = hT[:, q:q + EPP]
        src_lane = hT[:, q + EPP:q + EPP + EPP // 2].bitcast(f16)
        src_block = hT[:, q + EPP + EPP // 2:q + 2 * EPP].bitcast(f16)
        dst_lo = hT[:, q + 2 * EPP:q + 2 * EPP + EPP // 2].bitcast(f16)
        dst_hi = hT[:, q + 2 * EPP + EPP // 2:q + 3 * EPP].bitcast(f16)
        disorder = hT[:, q + 3 * EPP:q + 4 * EPP]
        q2 = q + 4 * EPP
        deg = hT[:, q2:q2 + HI]
        dinv = hT[:, q2 + 64:q2 + 64 + HI]
        t1 = hT[:, q2 + 128:q2 + 128 + HI]
        t2 = hT[:, q2 + 192:q2 + 192 + HI]
        t3 = hT[:, q2 + 256:q2 + 256 + HI]
        ones_t = hT[:, q2 + 320:q2 + 320 + HI]
        twice = hT[:, q2 + 384:q2 + 384 + P]
        lanes = hT[:, q2 + 514:q2 + 515]
        bad = hT[:, q2 + 545:q2 + 546]
        over = hT[0:1, q2 + 546:q2 + 547]
        ones1 = hT[:, q2 + 547:q2 + 548]
        starts_i = hT[:, q2 + 550:q2 + 550 + HI].bitcast(i32)
        factors = hT[:, q2 + 600:q2 + 600 + BLOCKS].bitcast(f16).rearrange("p (s a) -> p s a", s=2)
        below = hT[:, q2 + 626:q2 + 626 + LO]
        ones_sq = hT[:, q2 + 690:q2 + 690 + LO]
        sizes = hT[0:1, q2 + 754:q2 + 754 + NW]
        early_end = q2 + 754 + NW
        TILES = UN * WT
        wide = hT[:, NP:2 * NP].bitcast(f16)
        oh_src = wide[:, 0:2 * TILES * P].rearrange("p (b v n) -> p b v n", b=2, v=P)
        o = 2 * TILES * P
        oh_dst = wide[:, o:o + 2 * TILES * WIN].rearrange("p (b n v) -> p b n v", b=2, n=TILES)
        o += 2 * TILES * WIN
        sums32 = wide[:, o:o + 4 * TW_NODES].bitcast(f32).rearrange("p (b n) -> p b n", b=2)
        o += 4 * TW_NODES
        sums16 = wide[:, o:o + 2 * TW_NODES].rearrange("p (b n) -> p b n", b=2)
        o += 2 * TW_NODES
        assert o + TILES * WIN <= 2 * NP
        node_of = wide[:, 2 * NP - TILES * WIN:2 * NP]
        assert early_end <= 2 * NP - TILES * WIN // 2
        all_sums32 = wide[:, 0:2 * GCH].bitcast(f32)
        all_sums16 = wide[:, 2 * GCH:3 * GCH]

        work16 = work[:, :].bitcast(f16)
        oh_key = work16[:, 0:WDEEP * WT * WKEYS].rearrange("p (b k v) -> p b k v", b=WDEEP, k=WT)
        o = WDEEP * WT * WKEYS
        edge_buf = work16[:, o:o + 4 * TILES * TW].bitcast(f32).rearrange("p (h j k w) -> p h j k w", h=2, j=UN, k=WT)
        o += 4 * TILES * TW
        win_node = work16[:, o:o + 2 * NW].bitcast(f32)
        win_key = work16[:, o + 2 * NW:o + 4 * NW].bitcast(f32)
        starts_row = work16[0:1, o + 4 * NW:o + 6 * NW + 2].bitcast(i32)
        o += 6 * NW + 2
        lane_of = work16[:, o:o + LRUN * P].rearrange("p (v n) -> p v n", v=P)
        o += LRUN * P
        own_key = work16[:, o:o + 4 * TILES].bitcast(f32).rearrange("p (b n) -> p b n", b=2)
        o += 4 * TILES
        lane16 = work16[:, o:o + 2 * TILES].rearrange("p (b n) -> p b n", b=2)
        o += 2 * TILES
        turn_node = work16[:, o:o + 2 * TILES].rearrange("p (b n) -> p b n", b=2)
        o += 2 * TILES
        block_node = work16[:, o:o + 2 * BLOCKS].bitcast(f32)
        assert o + 2 * BLOCKS <= 2 * 3584 and TILES % LRUN == 0
        weights = work16[:, 0:8 * D].rearrange("p (s k n) -> p s k n", s=2, k=4)
        dst_factor = work[:, 4 * D:4 * D + CH]
        o = 4 * D + CH
        staged = work[:, o:o + 4 * D].rearrange("p (k n) -> p k n", k=4)
        linear = [work[:, o + g * 2 * CH:o + (g + 1) * 2 * CH].rearrange("p (f n) -> p f n", f=HALVES) for g in range(2)]
        summed = linear[1]

        banks = [ctx.enter_context(nc.psum_tensor(f"bank{n}", [P, 512], f32)) for n in range(8)]
        look_banks = banks[8 - LDEEP:]

        s_pads, s_src, s_dst, s_next, s_attr = (sem(n) for n in ("s_pads", "s_src", "s_dst", "s_next", "s_attr"))
        s_iota, s_ident0, s_ident = sem("s_iota"), sem("s_ident0"), sem("s_ident")
        s_dve1, s_codes, s_codes_out, s_bc = sem("s_dve1"), sem("s_codes"), sem("s_codes_out"), [sem(f"s_bc{n}") for n in range(3)]
        s_hist_oh, s_hist_mm, s_hist, s_deg, s_rep = (sem(n) for n in ("s_hist_oh", "s_hist_mm", "s_hist", "s_deg", "s_rep"))
        s_clamped, s_sqrt, s_factors = sem("s_clamped"), sem("s_sqrt"), sem("s_factors")
        s_starts, s_starts_out, s_starts_in = sem("s_starts"), sem("s_starts_out"), sem("s_starts_in")
        s_digits = sem("s_digits")
        s_bad, s_badsum = sem("s_bad"), sem("s_badsum")
        s_rowf, s_rowf_out = sem("s_rowf"), sem("s_rowf_out")
        s_match, s_look, s_oh_block, s_picked, s_reduced = (
            sem(n) for n in ("s_match", "s_look", "s_oh_block", "s_picked", "s_reduced"))
        s_weighed, s_attr_high, s_ewz = sem("s_weighed"), sem("s_attr_high"), sem("s_ewz")
        s_pads2, s_table, s_table_out = sem("s_pads2"), sem("s_table"), sem("s_table_out")

        def edges_in(eng, tile, flat, count, signal):
            full, rest = count // EPP, count % EPP
            eng.dma_start(tile[0:full], flat[0:full * EPP].rearrange("(p e) -> p e", e=EPP)).then_inc(signal, 16)
            eng.dma_start(tile[full:full + 1, 0:rest], flat[full * EPP:count].unsqueeze(0)).then_inc(signal, 16)

        with nc.Block() as block:
            @block.gpsimd
            def _(pool):
                nc.gpsimd.memset(next_i[96:P], PAD_DST)
                nc.gpsimd.memset(attr[96:P], 0.0).then_inc(s_pads2, 1)
                pool.wait_ge(s_pads2, 1)
                nc.gpsimd.memset(zeros16[:, :], 0.0)
                nc.gpsimd.iota(digit_of, [[1, LO], [0, HCH]], base=0, channel_multiplier=0,
                               allow_small_or_imprecise_dtypes=True).then_inc(s_digits, 1)
                nc.gpsimd.iota(block_of, [[1, BLOCKS], [0, LT]], base=0, channel_multiplier=0,
                               allow_small_or_imprecise_dtypes=True)
                nc.gpsimd.iota(lane_of, [[1, P], [0, LRUN]], base=0, channel_multiplier=0,
                               allow_small_or_imprecise_dtypes=True)
                nc.gpsimd.iota(node_of, [[WIN, UN], [0, WT], [1, WIN]], base=0, channel_multiplier=0,
                               allow_small_or_imprecise_dtypes=True)
                nc.gpsimd.iota(iota_row[:, :], [[1, max(GCH, WKEYS)]], base=0, channel_multiplier=0,
                               allow_small_or_imprecise_dtypes=True)
                nc.gpsimd.iota(lanes, [[0, 1]], base=0, channel_multiplier=1, allow_small_or_imprecise_dtypes=True)
                nc.gpsimd.iota(win_node, [[WIN, NW]], base=0, channel_multiplier=0,
                               allow_small_or_imprecise_dtypes=True)
                nc.gpsimd.iota(block_node, [[P, BLOCKS]], base=0, channel_multiplier=0,
                               allow_small_or_imprecise_dtypes=True)
                nc.gpsimd.iota(win_key, [[WKEYS, NW]], base=0, channel_multiplier=0,
                               allow_small_or_imprecise_dtypes=True).then_inc(s_iota, 1)
                nc.gpsimd.memset(ident[:, :], 0.0).then_inc(s_ident0, 1)
                pool.wait_ge(s_ident0, 1)
                nc.gpsimd.affine_select(out=ident[:, :], in_=ident[:, :], compare_op=ALU.not_equal, fill=1.0,
                                        base=0, pattern=[[-1, P]], channel_multiplier=1).then_inc(s_ident, 1)
                nc.gpsimd.memset(ew_cols[:, :, :, :], 0.0).then_inc(s_ewz, 1)
                for k in range(LTURNS):
                    pool.wait_ge(s_attr_high, k + 1)
                    some = slice(k * TURN_EDGES, (k + 1) * TURN_EDGES)
                    for s in range(2):
                        last = nc.gpsimd.tensor_tensor(table_attr[:, some, 1, s], attr[:, some], table_attr[:, some, 0, s],
                                                       ALU.subtract)
                    last.then_inc(s_table, 1)

            @block.sync
            def _(sp):
                sp.wait_ge(s_pads, 1)
                edges_in(sp, src_i, src, E, s_src)
                edges_in(sp, dst_i, dst, E, s_dst)
                sp.wait_ge(s_pads2, 1)
                edges_in(sp, next_i, dst[1:E], E - 1, s_next)
                sp.wait_ge(s_codes, 1)
                sp.dma_start(src_lane_dram.rearrange("(k p t) -> p k t", p=P, t=TURN_EDGES),
                             src_lane.rearrange("p (k t) -> p k t", t=TURN_EDGES)).then_inc(s_codes_out, 16)
                sp.wait_ge(s_codes_out, 16)
                for k in range(LTURNS):
                    some = slice(k * P * TURN_EDGES, (k + 1) * P * TURN_EDGES)
                    sp.dma_start(lane_bc[:, some], src_lane_dram[some].partition_broadcast(P)).then_inc(s_bc[min(k, 2)], 16)
                sp.dma_start(attr[0:ROWS], edge_attr[0:ROWS * EPP, :].rearrange("(p e) k -> p e k", e=EPP)
                             ).then_inc(s_attr, 16)
                sp.dma_start(attr[ROWS:ROWS + 1, 0:REST], edge_attr[ROWS * EPP:E, :].unsqueeze(0)).then_inc(s_attr, 16)
                sp.wait_ge(s_starts, 1)
                sp.dma_start(starts_dram.rearrange("(h l) -> l h", l=LO), starts_i[0:LO]).then_inc(s_starts_out, 16)
                sp.wait_ge(s_rowf, 1)
                sp.dma_start(dst_factor_dram.rearrange("(h l) -> l h", l=LO), t3[0:LO]).then_inc(s_rowf_out, 16)
                sp.wait_ge(s_starts_out, 16)
                sp.dma_start(starts_row, starts_dram[0:NW * WIN + 1:WIN].unsqueeze(0)).then_inc(s_starts_in, 16)
                for k in range(LTURNS):
                    sp.wait_ge(s_table, k + 1)
                    some = slice(k * TURN_EDGES, (k + 1) * TURN_EDGES)
                    sp.dma_start(edge_table.rearrange("(p e) w -> p e w", e=EPP)[:, some, :], table_tile[:, some, :]
                                 ).then_inc(s_table_out, 16)
                sp.wait_ge(s_starts_in, 16)
                sp.wait_ge(s_rowf_out, 16)
                sp.wait_ge(s_table_out, 16 * LTURNS)

            @block.vector
            def _(dve):
                steps = [0]

                def link(ins):
                    steps[0] += 1
                    ins.then_inc(s_dve1, 1)
                    dve.wait_ge(s_dve1, steps[0])

                nc.vector.memset(src_i[96:P], 0)
                nc.vector.memset(dst_i[96:P], PAD_DST).then_inc(s_pads, 1)
                dve.wait_ge(s_src, 32)
                link(nc.vector.tensor_scalar(tmp_i, src_i, P - 1, None, ALU.bitwise_and))
                nc.vector.tensor_copy(src_lane, tmp_i).then_inc(s_codes, 1)
                dve.wait_ge(s_codes, 1)
                link(nc.vector.tensor_copy(table_tile[:, :, 1], tmp_i))
                link(nc.vector.tensor_scalar(tmp_i, src_i, 7, None, ALU.logical_shift_right))
                link(nc.vector.tensor_copy(src_block, tmp_i))
                dve.wait_ge(s_dst, 32)
                link(nc.vector.tensor_scalar(tmp_i, dst_i, LO - 1, None, ALU.bitwise_and))
                link(nc.vector.tensor_copy(dst_lo, tmp_i))
                link(nc.vector.tensor_scalar(tmp_i, dst_i, 6, None, ALU.logical_shift_right))
                link(nc.vector.tensor_copy(dst_hi, tmp_i))
                dve.wait_ge(s_digits, 1)

                def hist(t0, b):
                    for oh, digit, size in ((oh_lo, dst_lo, LO), (oh_hi, dst_hi, HI)):
                        last = nc.vector.tensor_tensor(oh[:, b], digit_of[:, 0:size], digit[:, bass.ds(t0, HCH)]
                                                       .unsqueeze(1).broadcast_to([P, size, HCH]), ALU.is_equal)
                    last.then_inc(s_hist_oh, 1)
                for b in range(2):
                    hist(b * HCH, b)
                with dve.Fori(1, HSTEPS // 2) as k:
                    for b in range(2):
                        dve.wait_ge(s_hist_mm, 2 * k + b - 1)
                        hist((2 * k + b) * HCH, b)
                dve.wait_ge(s_iota, 1)
                link(nc.vector.tensor_copy(src_f, src_i))
                link(nc.vector.tensor_copy(dst_f, dst_i))
                nc.vector.scalar_tensor_tensor(table_tile[:, :, 0], dst_f, float(BLOCKS), src_block, ALU.mult, ALU.add)
                nc.vector.tensor_scalar(table_tile[:, :, 2], dst_f, NSCALE, None, ALU.mult)
                nc.vector.tensor_scalar(win_node, win_node, NSCALE, None, ALU.mult)
                nc.vector.tensor_scalar(node_of, node_of, NSCALE, None, ALU.mult)
                dve.wait_ge(s_next, 32)
                link(nc.vector.tensor_tensor(disorder, dst_i, next_i, ALU.is_gt))
                link(nc.vector.reduce_sum(bad, disorder, AX.X))
                nc.vector.memset(ones_t, 1.0)
                nc.vector.memset(ones1, 1.0)
                nc.vector.memset(one[:, :], 1.0)
                nc.vector.memset(dcol[:, :], 0.0)
                nc.vector.memset(ones_sq, 1.0)
                nc.vector.tensor_scalar(below[0:LO], iota_row[0:LO, 0:LO], lanes[0:LO], None, ALU.is_gt)
                nc.vector.tensor_scalar(sum_scale[:, :], lanes, float(LO + K_ATTR), 1.0 / DSCALE, ALU.is_ge, ALU.mult)
                link(nc.vector.tensor_scalar(high_sign[:, :], lanes, float(LO + K_ATTR), -2.0, ALU.is_ge, ALU.mult))
                link(nc.vector.tensor_scalar(high_sign[:, :], high_sign[:, :], 1.0, None, ALU.add))
                dve.wait_ge(s_ident, 1)
                nc.vector.tensor_copy(twice[0:LO, 0:LO], ident[0:LO, 0:LO])
                link(nc.vector.tensor_copy(twice[0:LO, LO:P], ident[0:LO, 0:LO]))

                def match(k, j):
                    size = P * TURN_EDGES // LDEEP
                    some = lane_bc[:, bass.ds(k * (LDEEP * size) + j * size, size)]
                    nc.vector.tensor_scalar(some, some, lanes, None, ALU.is_equal).then_inc(s_match, 1)
                for k in range(2):
                    dve.wait_ge(s_bc[k], 16)
                    for j in range(LDEEP):
                        match(k, j)
                dve.wait_ge(s_hist, 1)
                nc.vector.tensor_copy(t3[0:LO], banks[0][0:LO, 0:HI]).then_inc(s_deg, 1)
                dve.wait_ge(s_rep, 1)
                link(nc.vector.tensor_copy(deg, banks[1][:, 0:HI]))
                link(nc.vector.tensor_tensor_scan(t1[0:LO], ones_t[0:LO], banks[2][0:LO, 0:HI], 0.0, ALU.mult, ALU.add))
                link(nc.vector.tensor_tensor(t1[0:LO], t1[0:LO], banks[2][0:LO, 0:HI], ALU.subtract))
                link(nc.vector.tensor_tensor(t1[0:LO], t1[0:LO], banks[3][0:LO, 0:HI], ALU.add))
                nc.vector.tensor_copy(starts_i[0:LO], t1[0:LO]).then_inc(s_starts, 1)
                nc.vector.tensor_copy(bad, bad).then_inc(s_bad, 1)
                dve.wait_ge(s_starts, 1)
                nc.vector.tensor_scalar(t1, deg, 1.0, None, ALU.max).then_inc(s_clamped, 1)
                dve.wait_ge(s_clamped, 1)
                dve.wait_ge(s_sqrt, 1)
                link(nc.vector.reciprocal(dinv, t2))
                link(nc.vector.tensor_tensor(t3, dinv, dinv, ALU.mult))
                link(nc.vector.tensor_tensor(t3, t3, t1, ALU.mult))
                link(nc.vector.tensor_scalar(t3, t3, -0.5, 1.5, ALU.mult, ALU.add))
                link(nc.vector.tensor_tensor(dinv, dinv, t3, ALU.mult))
                link(nc.vector.tensor_scalar(t3, deg, 0.0, None, ALU.is_gt))
                link(nc.vector.tensor_tensor(dinv, dinv, t3, ALU.mult))
                nc.vector.tensor_scalar(t3, dinv, 1.0 / ZSCALE, None, ALU.mult).then_inc(s_rowf, 1)
                nc.vector.tensor_scalar(dcol[0:LO, 0:BLOCKS], dinv[0:LO, 0:HI:2], ZSCALE / (HMUL * WMUL), None, ALU.mult)
                link(nc.vector.tensor_scalar(dcol[LO:P, 0:BLOCKS - 1], dinv[LO:P, 1:HI:2], ZSCALE / (HMUL * WMUL), None, ALU.mult))
                to_lookup = DSCALE * HMUL * WMUL / ZSCALE
                link(nc.vector.tensor_scalar(factors[:, 0, :], dcol[:, :], to_lookup, None, ALU.mult))
                nc.vector.scalar_tensor_tensor(factors[:, 1, :], dcol[:, :], to_lookup, factors[:, 0, :], ALU.mult,
                                               ALU.subtract).then_inc(s_factors, 1)

                def block_onehot(n, b):
                    nc.vector.tensor_tensor(oh_block[:, b], block_of,
                                            src_block[:, bass.ds(n * LT, LT)].unsqueeze(1).broadcast_to([P, BLOCKS, LT]),
                                            ALU.is_equal).then_inc(s_oh_block, 1)

                def pick(n, b, first):
                    dve.wait_ge(s_oh_block, n + 1)
                    if not first:
                        dve.wait_ge(s_reduced, n - LDEEP + 1)
                    dve.wait_ge(s_look, n + 1)
                    nc.vector.tensor_tensor(picked[:, b], look_banks[b][:, 0:LT * BLOCKS].rearrange("p (t a) -> p t a", a=BLOCKS),
                                            oh_block[:, b].rearrange("p a t -> p t a"), ALU.mult).then_inc(s_picked, 1)

                def reduce(n, b):
                    dve.wait_ge(s_picked, n + 1)
                    nc.vector.reduce_sum(src_factor[:, bass.ds(n * LT, LT)], picked[:, b], AX.X).then_inc(s_reduced, 1)

                def weigh(k):
                    dve.wait_ge(s_reduced, (k + 1) * LDEEP)
                    some = attr[:, bass.ds(k * TURN_EDGES, TURN_EDGES)]
                    nc.vector.tensor_tensor(some, some, src_factor[:, bass.ds(k * TURN_EDGES, TURN_EDGES)].unsqueeze(2)
                                            .broadcast_to([P, TURN_EDGES, K_ATTR]), ALU.mult).then_inc(s_weighed, 1)

                def lookups(k, first, matching, last):
                    for j in range(LDEEP):
                        n = k * LDEEP + j
                        if matching:
                            match(k + 2, j)
                        if not (last and j == LDEEP - 1):
                            block_onehot(n + 1, (j + 1) % LDEEP)
                        pick(n, j, first)
                        if not (first and j == 0):
                            reduce(n - 1, (j - 1) % LDEEP)
                        if not first and j == 1:
                            weigh(k - 1)
                dve.wait_ge(s_attr, 32)
                block_onehot(0, 0)
                dve.wait_ge(s_bc[2], 16 * (LTURNS - 2))
                lookups(0, True, True, False)
                with dve.Fori(1, LTURNS - 2) as k:
                    lookups(k, False, True, False)
                lookups(LTURNS - 2, False, False, False)
                lookups(LTURNS - 1, False, False, True)
                reduce(LSTEPS - 1, LDEEP - 1)
                weigh(LTURNS - 1)
                dve.wait_ge(s_badsum, 1)
                dve.wait_ge(s_starts_in, 16)
                link(nc.vector.tensor_tensor(sizes, starts_row[:, 1:NW + 1], starts_row[:, 0:NW], ALU.subtract))
                link(nc.vector.tensor_scalar(sizes, sizes, float(CAP), None, ALU.is_gt))
                link(nc.vector.reduce_sum(over, sizes, AX.X))
                nc.vector.tensor_tensor(flag_row[:, :], over, banks[4][0:1, HI:HI + 1], ALU.add)

            @block.scalar
            def _(act):
                act.wait_ge(s_clamped, 1)
                nc.scalar.activation(t2, t1, ACT.Sqrt).then_inc(s_sqrt, 1)
                for k in range(LTURNS):
                    act.wait_ge(s_weighed, k + 1)
                    some = slice(k * TURN_EDGES, (k + 1) * TURN_EDGES)
                    nc.scalar.copy(table_attr[:, some, 0], attr[:, some].unsqueeze(2).broadcast_to([P, TURN_EDGES, 2, K_ATTR])
                                   ).then_inc(s_attr_high, 1)

            @block.tensor
            def _(pe):
                pe.wait_ge(s_digits, 1)
                nc.tensor.matmul(banks[0][0:LO, 0:HI], zeros16[:, 0:LO], zeros16[:, 0:HI], start=True, stop=False)
                with pe.Fori(0, HSTEPS // 2) as k:
                    for b in range(2):
                        pe.wait_ge(s_hist_oh, 2 * k + b + 1)
                        for t in range(HCH):
                            last = nc.tensor.matmul(banks[0][0:LO, 0:HI], oh_lo[:, b, :, t], oh_hi[:, b, :, t],
                                                    start=False, stop=False)
                        last.then_inc(s_hist_mm, 1)
                nc.tensor.matmul(banks[0][0:LO, 0:HI], zeros16[:, 0:LO], zeros16[:, 0:HI], start=False,
                                 stop=True).then_inc(s_hist, 1)
                pe.wait_ge(s_deg, 1)
                nc.tensor.matmul(banks[1][:, 0:HI], twice[0:LO, :], t3[0:LO], start=True, stop=True)
                nc.tensor.matmul(banks[2][0:LO, 0:HI], ones_sq[0:LO], t3[0:LO], start=True, stop=True)
                nc.tensor.matmul(banks[3][0:LO, 0:HI], below[0:LO], t3[0:LO], start=True, stop=True).then_inc(s_rep, 1)
                pe.wait_ge(s_bad, 1)
                nc.tensor.matmul(banks[4][0:1, HI:HI + 1], bad, ones1, start=True, stop=True).then_inc(s_badsum, 1)
                pe.wait_ge(s_factors, 1)

                def looks(k, first):
                    pe.wait_ge(s_match, LDEEP * (k + 1))
                    for j in range(LDEEP):
                        n = k * LDEEP + j
                        if not first:
                            pe.wait_ge(s_picked, n - LDEEP + 1)
                        for t in range(LT):
                            edges = lane_bc3[:, bass.ds(k * P, P), j * LT + t]
                            for s in range(2):
                                last = nc.tensor.matmul(look_banks[j][:, t * BLOCKS:(t + 1) * BLOCKS], edges,
                                                        factors[:, s, :], start=(s == 0), stop=(s == 1))
                        last.then_inc(s_look, 1)
                looks(0, True)
                with pe.Fori(1, LTURNS) as k:
                    looks(k, False)

        s_edges = [[sem(f"s_edges{h}{j}") for j in range(UN)] for h in range(2)]
        s_onehots, s_window, s_taken, s_keys = sem("s_onehots"), sem("s_window"), sem("s_taken"), sem("s_keys")
        s_all_oh, s_all_mm, s_all_block, s_all_taken = (sem(n) for n in ("s_all_oh", "s_all_mm", "s_all_block", "s_all_taken"))
        s_high, s_sums, s_rows, s_x, s_cleared = sem("s_high"), sem("s_sums"), sem("s_rows"), sem("s_x"), sem("s_cleared")
        s_distance, s_squares, s_oh_dst = sem("s_distance"), sem("s_squares"), sem("s_oh_dst")
        s_aff, s_ew, s_all_attr = sem("s_aff"), sem("s_ew"), sem("s_all_attr")
        s_ln_cleared, s_ln_step, s_ln_mean = (sem(n) for n in ("s_ln_cleared", "s_ln_step", "s_ln_mean"))

        def x_in(eng, tiles, signal):
            eng.dma_start(tiles[:, 0:BLOCKS - 1], x[0:(BLOCKS - 1) * P, :].rearrange("(i p) f -> p i f", p=P)).then_inc(signal, 16)
            eng.dma_start(tiles[0:TAIL, BLOCKS - 1], x[(BLOCKS - 1) * P:N, :]).then_inc(signal, 16)

        with nc.Block() as block:
            @block.sync
            def _(sp):
                irregular = sp.value_load(flag_row[0:1, 0:1])
                with sp.If(irregular > 0):
                    sp.wait_ge(s_all_block, BLOCKS + 1)
                    x_in(sp, x_tiles, s_x)
                with sp.Else():
                    def fetch(k, half, first):
                        _, starts = nc.values_load_multi_w_load_instructions(
                            starts_row[0:1, bass.ds(UN * k, UN)], engines=[sp.engine], min_val=0, max_val=E,
                            skip_runtime_bounds_check_because="a start is a count of some of the E edges")
                        for j, start in enumerate(starts):
                            w = UN * k + j
                            if not first:
                                sp.wait_ge(s_window, w - 2 * UN + 1)
                            sp.dma_start(edge_buf[:, half, j].rearrange("p k w -> p (k w)"),
                                         edge_table[bass.ds(start, CAP), :].rearrange("(p k) w -> p (k w)", k=WT)
                                         ).then_inc(s_edges[half][j], 16)
                    fetch(0, 0, True)
                    fetch(1, 1, True)
                    x_in(sp, x_tiles, s_x)
                    with sp.Fori(1, TURNS // 2) as k:
                        fetch(2 * k, 0, False)
                        fetch(2 * k + 1, 1, False)
                    fetch(TURNS - 1, 0, False)
                for n, v in enumerate((mlp_b, bn_g, bn_b)):
                    sp.dma_start(aff[:, n, :], v.rearrange("l (f p) -> p (l f)", p=P)).then_inc(s_aff, 16)
                sp.wait_ge(s_ewz, 1)
                for s in range(2):
                    k = K_ATTR * s
                    sp.dma_start(ew_cols[:, :, 0, k + 3], ew1.rearrange("l k p -> p (l k)")).then_inc(s_ew, 16)
                    for j in range(K_ATTR - 1):
                        sp.dma_start(ew_cols[:, :, 1, k + j], ew2[:, j, :].rearrange("l p -> p l")).then_inc(s_ew, 16)
                sp.wait_ge(s_aff, 48)
                sp.wait_ge(s_ew, 16 * 2 * K_ATTR)

            @block.gpsimd
            def _(pool):
                def rows(n, node0, size, both16, both32):
                    pool.wait_ge(s_sums, n + 1)
                    nc.gpsimd.tensor_tensor(counts3[EWR, BLOCKS - 1, bass.ds(node0, size)], both32[EWR], both16[EWR],
                                            ALU.add).then_inc(s_rows, 1)
                nc.gpsimd.memset(ln_sums[:, :], 0.0).then_inc(s_ln_cleared, 1)
                pool.wait_ge(s_ln_cleared, 1)
                irregular = pool.value_load(flag_row[0:1, 0:1])
                with pool.If(irregular > 0):
                    for c in range(NG):
                        rows(c, c * GCH, GCH, all_sums16, all_sums32)
                with pool.Else():
                    nc.gpsimd.memset(counts3[:, :, NW * WIN:NP], 0.0).then_inc(s_cleared, 1)
                    pool.wait_ge(s_cleared, 1)

                    def dst_distances(k, b, turn):
                        for j in range(UN):
                            pool.wait_ge(s_edges[b][j], 16 * turn + 16)
                        nc.gpsimd.tensor_tensor(turn_node[:, b], edge_buf[:, b].rearrange("p j t w -> p (j t) w")[:, :, 2],
                                                win_node[:, bass.ds(UN * k, 1)].broadcast_to([P, TILES]), ALU.subtract
                                                ).then_inc(s_distance, 1)
                        pool.wait_ge(s_distance, 2 * k + 1)
                        nc.gpsimd.tensor_tensor(oh_dst[:, b], turn_node[:, b].unsqueeze(2).broadcast_to([P, TILES, WIN]),
                                                node_of.rearrange("p (n v) -> p n v", v=WIN), ALU.subtract
                                                ).then_inc(s_distance, 1)
                        pool.wait_ge(s_distance, 2 * k + 2)
                        nc.gpsimd.tensor_tensor(oh_dst[:, b], oh_dst[:, b], oh_dst[:, b], ALU.mult).then_inc(s_squares, 1)

                    def rows_of_turn(k, b):
                        pool.wait_ge(s_squares, min(k + 2, TURNS) if isinstance(k, int) else k + 2)
                        rows(k, k * TW_NODES, TW_NODES, sums16[:, b], sums32[:, b])
                        pool.wait_ge(s_rows, k + 1)
                    dst_distances(0, 0, 0)
                    dst_distances(1, 1, 0)
                    with pool.Fori(0, TURNS // 2 - 1) as k:
                        for b in range(2):
                            rows_of_turn(2 * k + b, b)
                            dst_distances(2 * k + b + 2, b, k + 1)
                    rows_of_turn(TURNS - 3, 0)
                    dst_distances(TURNS - 1, 0, TURNS // 2)
                    rows_of_turn(TURNS - 2, 1)
                    rows_of_turn(TURNS - 1, 0)

            @block.vector
            def _(dve):
                irregular = dve.value_load(flag_row[0:1, 0:1])
                with dve.If(irregular > 0):
                    def all_edges(first, t, node0):
                        dve.wait_ge(s_all_mm, first)
                        for c in range(NG):
                            last = nc.vector.tensor_scalar(all_dst[:, c * GCH:(c + 1) * GCH], iota_row[:, 0:GCH], float(c * GCH),
                                                           dst_f[:, bass.ds(t, 1)], ALU.add, ALU.is_equal)
                        if node0 is not None:
                            last = nc.vector.tensor_scalar(all_src, iota_row[:, 0:P], node0,
                                                           src_f[:, bass.ds(t, 1)], ALU.add, ALU.is_equal)
                        else:
                            last = nc.vector.tensor_copy(all_attr, attr16[:, bass.ds(t, 1), :].rearrange("p o k -> p (o k)"))
                        last.then_inc(s_all_oh, 1)
                    with dve.Fori(0, BLOCKS) as a:
                        with dve.Fori(0, EPP) as t:
                            all_edges(a * EPP + t + 1, t, block_node[:, bass.ds(a, 1)])
                    twice_attr = attr.unsqueeze(2).broadcast_to([P, EPP, 2, K_ATTR])
                    high, low = (attr16[:, :, 2 * K_ATTR * v:2 * K_ATTR * (v + 1)].rearrange("p e (s k) -> p e s k", s=2)
                                 for v in range(2))
                    nc.vector.tensor_copy(high, twice_attr).then_inc(s_all_attr, 1)
                    dve.wait_ge(s_all_attr, 1)
                    nc.vector.tensor_tensor(low, twice_attr, high, ALU.subtract).then_inc(s_all_attr, 1)
                    dve.wait_ge(s_all_attr, 2)
                    with dve.Fori(0, EPP) as t:
                        all_edges(BLOCKS * EPP + t + 1, t, None)
                with dve.Else():
                    def onehots(k, b, turn, first):
                        flat = edge_buf[:, b].rearrange("p j t w -> p (j t) w")
                        if not first:
                            dve.wait_ge(s_window, UN * (k - 1))
                        for j in range(UN):
                            dve.wait_ge(s_edges[b][j], 16 * turn + 16)
                        nc.vector.tensor_tensor(own_key[:, b].rearrange("p (j t) -> p j t", j=UN), edge_buf[:, b, :, :, 0],
                                                win_key[:, bass.ds(UN * k, UN)].unsqueeze(2).broadcast_to([P, UN, WT]),
                                                ALU.subtract)
                        nc.vector.tensor_copy(lane16[:, b], flat[:, :, 1]).then_inc(s_keys, 1)
                        dve.wait_ge(s_keys, k + 1)
                        runs = TILES // LRUN
                        nc.vector.tensor_tensor(oh_src[:, b].rearrange("p v (q n) -> p v q n", q=runs),
                                                lane_of.unsqueeze(2).broadcast_to([P, P, runs, LRUN]),
                                                lane16[:, b].rearrange("p (q n) -> p q n", q=runs).unsqueeze(1)
                                                .broadcast_to([P, P, runs, LRUN]), ALU.is_equal)
                        for j in range(UN):
                            if not (first and b == 0 and j < WDEEP):
                                dve.wait_ge(s_window, UN * k + j - WDEEP + 1)
                            for t in range(WT):
                                n = WT * j + t
                                last = nc.vector.tensor_scalar(oh_key[:, j % WDEEP, t, :], iota_row[:, 0:WKEYS],
                                                               own_key[:, b, n:n + 1], None, ALU.is_equal)
                            last.then_inc(s_onehots, 1)
                    onehots(0, 0, 0, True)
                    onehots(1, 1, 0, True)
                    with dve.Fori(1, TURNS // 2) as k:
                        onehots(2 * k, 0, k, False)
                        onehots(2 * k + 1, 1, k, False)
                    onehots(TURNS - 1, 0, TURNS // 2, False)

            @block.tensor
            def _(pe):
                irregular = pe.value_load(flag_row[0:1, 0:1])
                with pe.If(irregular > 0):
                    def all_edges(base, parts, rows):
                        count = rows.stop - rows.start
                        for c in range(NG):
                            nc.tensor.matmul(banks[c][rows, 0:GCH], zeros16[:, 0:count], zeros16[:, :], start=True, stop=False)
                        with pe.Fori(0, EPP) as t:
                            pe.wait_ge(s_all_oh, base + t + 1)
                            for w in parts:
                                for c in range(NG):
                                    last = nc.tensor.matmul(banks[c][rows, 0:GCH], w, all_dst[:, c * GCH:(c + 1) * GCH],
                                                            start=False, stop=False)
                            last.then_inc(s_all_mm, 1)
                        for c in range(NG):
                            last = nc.tensor.matmul(banks[c][rows, 0:GCH], zeros16[:, 0:count], zeros16[:, :], start=False, stop=True)
                        last.then_inc(s_all_block, 1)
                    pe.sem_inc(s_all_mm, 1)
                    with pe.Fori(0, BLOCKS) as a:
                        pe.wait_ge(s_all_taken, a + 1)
                        all_edges(a * EPP, [all_src], slice(0, P))
                    pe.wait_ge(s_all_taken, BLOCKS + 1)
                    all_edges(BLOCKS * EPP, [all_attr[:, 2 * K_ATTR * s:2 * K_ATTR * (s + 1)] for s in range(2)], EWR)
                with pe.Else():
                    def products(k, half, first):
                        for j in range(UN):
                            w = UN * k + j
                            b = j % WDEEP
                            pe.wait_ge(s_onehots, w + 1)
                            if not (first and k == 0 and j < WDEEP):
                                pe.wait_ge(s_taken, w - WDEEP + 1)
                            if j == 0 and not first:
                                pe.wait_ge(s_sums, k - 1)
                            for t in range(WT):
                                n = WT * j + t
                                nc.tensor.matmul(banks[b][:, 0:WKEYS], oh_src[:, half, :, n], oh_key[:, b, t, :],
                                                 start=(t == 0), stop=(t == WT - 1))
                            if j == 0:
                                pe.wait_ge(s_oh_dst, k + 1)
                            for t in range(WT):
                                n = WT * j + t
                                a16 = edge_buf[:, half, j, t, 3:TW].bitcast(f16)
                                for s in range(2):
                                    last = nc.tensor.matmul(banks[4 + half][EWR, j * WIN:(j + 1) * WIN],
                                                            a16[:, 2 * K_ATTR * s:2 * K_ATTR * (s + 1)],
                                                            oh_dst[:, half, n, :], start=(t == 0 and s == 0),
                                                            stop=(t == WT - 1 and s == 1))
                            last.then_inc(s_window, 1)
                    products(0, 0, True)
                    products(1, 1, True)
                    with pe.Fori(1, TURNS // 2) as k:
                        products(2 * k, 0, False)
                        products(2 * k + 1, 1, False)
                    products(TURNS - 1, 0, False)

            @block.scalar
            def _(act):
                def ln_total(i, n, place):
                    tile = x_tiles[0:n, bass.ds(i, 1)].rearrange("p i f -> p (i f)")
                    nc.scalar.activation(banks[6 + place][0:n, 0:D], tile, ACT.Copy,
                                         accum_out=ln_sum[0:n, bass.ds(i, 1)]).then_inc(s_ln_step, 1)

                def ln_squares(i, n, place):
                    tile = x_tiles[0:n, bass.ds(i, 1)].rearrange("p i f -> p (i f)")
                    nc.scalar.activation(banks[6 + place][0:n, 0:D], tile, ACT.Square, bias=ln_minus_mean[0:n, bass.ds(i, 1)],
                                         accum_out=ln_square[0:n, bass.ds(i, 1)]).then_inc(s_ln_step, 1)

                def ln_means():
                    act.wait_ge(s_ln_step, BLOCKS)
                    ln_total(BLOCKS - 1, TAIL, 0)
                    act.wait_ge(s_ln_step, BLOCKS + 1)
                    nc.scalar.mul(ln_minus_mean, ln_sum, -1.0 / D).then_inc(s_ln_mean, 1)
                    act.wait_ge(s_ln_mean, 1)

                def two_parts(n, sums, both16, both32):
                    nc.scalar.mul(both16[EWR], sums, 1.0 / DSCALE).then_inc(s_high, 1)
                    nc.scalar.activation(both32[EWR], sums, ACT.Copy, scale=sum_scale[EWR, :])
                    act.wait_ge(s_high, n + 1)
                    nc.scalar.activation(both16[EWR], both16[EWR], ACT.Copy, scale=high_sign[EWR, :]).then_inc(s_sums, 1)
                irregular = act.value_load(flag_row[0:1, 0:1])
                with act.If(irregular > 0):
                    act.sem_inc(s_all_taken, 1)
                    with act.Fori(0, BLOCKS) as a:
                        act.wait_ge(s_all_block, a + 1)
                        for c in range(NG):
                            last = nc.scalar.copy(countsT[:, bass.ds(a * NP + c * GCH, GCH)], banks[c][:, 0:GCH])
                        last.then_inc(s_all_taken, 1)
                    act.wait_ge(s_all_block, BLOCKS + 1)
                    for c in range(NG):
                        if c > 0:
                            act.wait_ge(s_rows, c)
                        two_parts(c, banks[c][EWR, 0:GCH], all_sums16, all_sums32)
                    act.wait_ge(s_x, 32)
                    act.wait_ge(s_ln_cleared, 1)
                    act.sem_inc(s_ln_step, 1)
                    act.wait_ge(s_sums, NG)
                    for i in range(BLOCKS - 1):
                        act.wait_ge(s_ln_step, i + 1)
                        ln_total(i, P, 0)
                    ln_means()
                    for i in range(BLOCKS):
                        act.wait_ge(s_ln_step, BLOCKS + i + 1)
                        ln_squares(i, P if i < BLOCKS - 1 else TAIL, 0)
                with act.Else():
                    def dst_onehots(k, half):
                        act.wait_ge(s_squares, k + 1)
                        nc.scalar.activation(oh_dst[:, half], oh_dst[:, half], ACT.Relu, bias=one[:, :],
                                             scale=-1.0 / NSCALE ** 2
                                             ).then_inc(s_oh_dst, 1)

                    def turn(k, half, first, done=None, last=False):
                        if done is not None:
                            act.wait_ge(s_ln_step, done)
                        for j in range(UN):
                            w = UN * k + j
                            act.wait_ge(s_window, w + 1)
                            nc.scalar.copy(counts3[:, :, bass.ds(w * WIN, WIN)],
                                           banks[j % WDEEP][:, 0:WKEYS].rearrange("p (d a) -> p a d", a=BLOCKS)
                                           ).then_inc(s_taken, 1)
                            if j == UN // 2 and not last:
                                dst_onehots(k + 1, 1 - half)
                        if not first:
                            act.wait_ge(s_rows, k - 1)
                        two_parts(k, banks[4 + half][EWR, 0:TW_NODES], sums16[:, half], sums32[:, half])

                    def turns(first, of_each, before):
                        with act.Fori(first // 2, (first + LN_TURNS) // 2) as k:
                            for half in range(2):
                                i = (2 * k + half - first) * LNB
                                turn(2 * k + half, half, False, i + before)
                                for m in range(LNB):
                                    of_each(i + m, P, m)
                    act.sem_inc(s_ln_step, 1)
                    dst_onehots(0, 0)
                    turn(0, 0, True)
                    turn(1, 1, True)
                    act.wait_ge(s_x, 32)
                    act.wait_ge(s_ln_cleared, 1)
                    turns(LN_FIRST, ln_total, 1)
                    ln_means()
                    turns(LN_FIRST + LN_TURNS, ln_squares, BLOCKS + 1)
                    act.wait_ge(s_ln_step, 2 * BLOCKS)
                    ln_squares(BLOCKS - 1, TAIL, 0)
                    for k in range(LN_FIRST + 2 * LN_TURNS, TURNS):
                        turn(k, k % 2, False, last=(k == TURNS - 1))

        s_hn, s_lnz = [sem("s_hn_even"), sem("s_hn_odd")], sem("s_lnz")
        s_chain, s_var, s_root, s_ln = (sem(n) for n in ("s_chain", "s_var", "s_root", "s_ln"))
        s_h0T, s_h0hi, s_norm = (sem(n) for n in ("s_h0T", "s_h0hi", "s_norm"))
        s_final = [sem("s_final0"), sem("s_final1")]
        s_w, s_whi, s_wparts, s_ewnow, s_eww, s_ewhi, s_ewparts = (
            sem(n) for n in ("s_w", "s_whi", "s_wparts", "s_ewnow", "s_eww", "s_ewhi", "s_ewparts"))
        s_linear, s_hhi, s_msg, s_hi, s_parts = (sem(n) for n in ("s_linear", "s_hhi", "s_msg", "s_hi", "s_parts"))
        s_sum = [sem("s_sum0"), sem("s_sum1")]
        s_scaled = [sem("s_scaled0"), sem("s_scaled1")]
        s_df, s_own, s_comb, s_relu = (sem(n) for n in ("s_df", "s_own", "s_comb", "s_relu"))
        s_bnvar, s_bnroot, s_affine = sem("s_bnvar"), sem("s_bnroot"), sem("s_affine")
        s_xr = [sem(f"s_xr{g}") for g in range(NBQ)]
        s_back, s_res, s_out = sem("s_back"), sem("s_res"), sem("s_out")

        ln_v, ln_r, ln_t, ln_b = (mv[:, BLOCKS * n:BLOCKS * (n + 1)] for n in range(4))
        stats4 = stats[:, :].rearrange("p (f c s) -> p f c s", f=HALVES, s=6)
        bn_mv = small[:, 0:4].rearrange("p (f v) -> p f v", f=HALVES)
        bn_v, bn_r, bn_t, bn_scale, bn_shift = (small[:, 4 + 2 * n:6 + 2 * n] for n in range(5))
        bias_now = small[:, 14:16]
        x_again = countsT[:, 0:2 * BLOCKS * D].bitcast(f32).rearrange("p (i f) -> p i f", i=BLOCKS)
        out_tiles = countsT[:, 2 * BLOCKS * D:4 * BLOCKS * D].bitcast(f32).rearrange("p (i f) -> p i f", i=BLOCKS)
        hT16 = hT[:, :].bitcast(f16)
        PASSES = [(0, 0), (0, 1), (1, 0)]

        def nodes(i):
            return P if i < BLOCKS - 1 else TAIL

        def width(c):
            return TAIL_CH if isinstance(c, int) and c == LAST else CH

        def part(f, s, c, at, n):
            return hT16[:, bass.ds(2 * CH * c + (2 * f * NP + s * width(c) + at), n)]

        def parts(s, c, at, n):
            return hT16.rearrange("p (f m) -> p f m", f=HALVES)[:, :, bass.ds(2 * CH * c + s * width(c) + at, n)]

        PIECES = [(0, 0, P), (0, P, CH - P)] + [(c, 0, width(c)) for c in range(1, NCH)]

        def block_piece(i):
            return {0: 0, 1: 1}.get(i, i // CB + 1 if i % CB == 0 else None)

        def both_halves(i, n):
            return banks[2 + i % TB][:, 0:HALVES * P].rearrange("p (f m) -> p f m", f=HALVES)[:, :, 0:n]

        def group(g):
            return range(g * CB, min((g + 1) * CB, BLOCKS))

        with nc.Block() as block:
            @block.sync
            def _(sp):
                def weights_in(l):
                    sp.dma_start(staged, mlp_w[bass.ds(l, 1)].rearrange("l (k p) n -> p (l k) n", p=P)).then_inc(s_w, 16)
                weights_in(0)
                def factors_in(n, c):
                    sp.wait_ge(s_scaled[1], n + 1)
                    sp.dma_start(dst_factor[:, 0:width(c)], dst_factor_dram[bass.ds(c * CH, width(c))].partition_broadcast(P)
                                 ).then_inc(s_df, 16)

                def layer(l, more):
                    factors_in(l * NCH, 0)
                    if more:
                        sp.wait_ge(s_norm, (l + 1) * NPC)
                        sp.wait_ge(s_wparts, l + 1)
                        sp.wait_ge(s_eww, l + 1)
                        weights_in(l + 1)
                    with sp.Fori(1, LAST) as c:
                        factors_in(l * NCH + c, c)
                    factors_in(l * NCH + LAST, LAST)
                with sp.Fori(0, L - 1) as l:
                    layer(l, True)
                layer(L - 1, False)
                sp.wait_ge(s_sum[1], L * NCH)
                for g in range(NBQ):
                    i0, i1 = g * BQ, min((g + 1) * BQ, BLOCKS - 1)
                    sp.dma_start(x_again[:, i0:i1], x[i0 * P:i1 * P, :].rearrange("(i p) f -> p i f", p=P)).then_inc(s_xr[g], 16)
                sp.dma_start(x_again[0:TAIL, BLOCKS - 1], x[(BLOCKS - 1) * P:N, :]).then_inc(s_xr[NBQ - 1], 16)
                for g in range(NBQ):
                    i0, i1 = g * BQ, (g + 1) * BQ
                    sp.wait_ge(s_res, i1)
                    if i1 == BLOCKS:
                        i1 -= 1
                        sp.dma_start(out[i1 * P:N, :], out_tiles[0:TAIL, i1]).then_inc(s_out, 16)
                    sp.dma_start(out[i0 * P:i1 * P, :].rearrange("(i p) f -> p i f", p=P), out_tiles[:, i0:i1]).then_inc(s_out, 16)
                sp.wait_ge(s_out, 16 * (NBQ + 1))

            @block.vector
            def _(dve):
                steps = [0]

                def link(ins):
                    steps[0] += 1
                    ins.then_inc(s_chain, 1)
                    dve.wait_ge(s_chain, steps[0])

                def newton(v, r, t, times, to, chain):
                    chain(nc.vector.reciprocal(r, r))
                    chain(nc.vector.scalar_tensor_tensor(t, r, -0.5, v, ALU.mult, ALU.mult))
                    chain(nc.vector.tensor_tensor(t, t, r, ALU.mult))
                    if isinstance(times, float):
                        chain(nc.vector.tensor_scalar(t, t, 1.5, times, ALU.add, ALU.mult))
                    else:
                        chain(nc.vector.scalar_tensor_tensor(t, t, 1.5, times, ALU.add, ALU.mult))
                    chain(nc.vector.tensor_tensor(to, t, r, ALU.mult))

                nc.vector.tensor_scalar(ln_v, ln_square, 1.0 / D, EPS, ALU.mult, ALU.add).then_inc(s_var, 1)
                dve.wait_ge(s_var, 1)
                dve.wait_ge(s_root, 1)
                newton(ln_v, ln_r, ln_t, HMUL, ln_r, link)
                nc.vector.tensor_tensor(ln_b, ln_minus_mean, ln_r, ALU.mult).then_inc(s_ln, 1)
                dve.wait_ge(s_ln, 1)
                link(nc.vector.tensor_scalar(aff[:, 1:3, 0:HALVES * (L - 1)], aff[:, 1:3, 0:HALVES * (L - 1)], HMUL, None, ALU.mult))

                def split_weights(l):
                    dve.wait_ge(s_whi, l + 1)
                    nc.vector.scalar_tensor_tensor(weights[:, 1], staged, WMUL, weights[:, 0], ALU.mult,
                                                   ALU.subtract).then_inc(s_wparts, 1)
                    nc.vector.tensor_copy(ew_now[:, :, :].rearrange("p f k -> p (f k)"),
                                          ew_cols[:, bass.ds(l, 1)].rearrange("p l f k -> p (l f k)")).then_inc(s_ewnow, 1)
                for i in range(BLOCKS + TB):
                    if i < BLOCKS and i % 2:
                        nc.vector.tensor_scalar(x_tiles[0:nodes(i), i], x_tiles[0:nodes(i), i], ln_r[0:nodes(i), i:i + 1],
                                                ln_b[0:nodes(i), i:i + 1], ALU.mult, ALU.add).then_inc(s_hn[1], 1)
                    if i >= TB:
                        j = i - TB
                        n, c = nodes(j), j // CB
                        dve.wait_ge(s_h0hi, j + 1)
                        nc.vector.scalar_tensor_tensor(parts(1, c, (j % CB) * P, n), both_halves(j, n), 0.0,
                                                       parts(0, c, (j % CB) * P, n), ALU.max, ALU.subtract).then_inc(s_lnz, 1)
                    if i == BLOCKS // 2 + 4:
                        split_weights(0)
                nc.vector.memset(parts(0, LAST, TAIL, TAIL_CH - TAIL), 0.0)
                link(nc.vector.memset(parts(1, LAST, TAIL, TAIL_CH - TAIL), 0.0))
                dve.sem_inc(s_norm, NPC)
                dve.wait_ge(s_lnz, BLOCKS)
                nc.vector.memset(hs4[:, BLOCKS - 1], 0.0).then_inc(s_lnz, 1)
                for h in range(2):
                    dve.sem_inc(s_scaled[h], 1)
                base = steps[0]
                CHAIN = 9

                def low_messages(l, i):
                    dve.wait_ge(s_hi, l * BLOCKS + i + 1)
                    n = nodes(i)
                    nc.vector.scalar_tensor_tensor(hs4[0:n, i, 1], banks[4 + i % MB][0:n, 0:D], dcol[0:n, i:i + 1],
                                                   hs4[0:n, i, 0], ALU.mult, ALU.subtract).then_inc(s_parts, 1)

                def low_edge_weights(l):
                    dve.wait_ge(s_ewhi, l + 1)
                    nc.vector.scalar_tensor_tensor(hs4[EWR, BLOCKS - 1, 1], banks[7][EWR, 0:D], ZSCALE,
                                                   hs4[EWR, BLOCKS - 1, 0], ALU.mult, ALU.subtract).then_inc(s_ewparts, 1)

                def affine(l, q):
                    g, at, n = PIECES[q]
                    if q >= 3:
                        dve.wait_ge(s_norm, l * NPC + q - 1)
                    for f in range(HALVES):
                        last = nc.vector.tensor_scalar(linear[g % 2][:, f, at:at + n],
                                                       hT3[:, f, g * CH + at:g * CH + at + n], bn_scale[:, f:f + 1],
                                                       bn_shift[:, f:f + 1], ALU.mult, ALU.add)
                    last.then_inc(s_linear, 1)

                def low_features(l, q):
                    g, at, n = PIECES[q]
                    if q == 0:
                        dve.wait_ge(s_linear, (l - 1) * NPC + 2)
                    dve.wait_ge(s_hhi, (l - 1) * NPC + q + 1)
                    nc.vector.scalar_tensor_tensor(parts(1, g, at, n), linear[g % 2][:, :, at:at + n], 0.0,
                                                   parts(0, g, at, n), ALU.max, ALU.subtract).then_inc(s_norm, 1)

                def layer(l, first, more):
                    if not first:
                        dve.wait_ge(s_eww, l + 1)
                        for q in range(2):
                            affine(l, q)
                    nc.vector.tensor_copy(bias_now, aff[:, 0, bass.ds(l * HALVES, HALVES)])
                    if not first:
                        low_features(l, 0)
                        low_features(l, 1)
                        affine(l, 2)
                    for i in range(BLOCKS):
                        low_messages(l, i)
                        g = i // CB
                        if i == CB:
                            low_edge_weights(l)
                        if not first and i % CB == 0 and g + 2 < NPC:
                            low_features(l, g + 2)
                        if not first and i % CB == 2 and g + 3 < NPC:
                            affine(l, g + 3)

                    def combine(n, c, h, tops):
                        w = width(c)
                        dve.wait_ge(s_sum[h], n + 1)
                        dve.wait_ge(s_relu, 2 * n + h + 1)
                        if h == 0:
                            dve.wait_ge(s_df, 16 * n + 16)
                        nc.vector.tensor_tensor(summed[:, h, 0:w], banks[h][:, 0:w], dst_factor[:, 0:w],
                                                ALU.mult).then_inc(s_scaled[h], 1)
                        dve.wait_ge(s_scaled[h], n + 2)
                        dve.wait_ge(s_own, tops)
                        own = banks[6][:, h * LO:h * LO + w] if w < CH else banks[2 + h][:, 0:w]
                        nc.vector.scalar_tensor_tensor(summed[:, h, 0:w], own, 1.0 / (HMUL * WMUL), summed[:, h, 0:w],
                                                       ALU.mult, ALU.add).then_inc(s_comb, 1)

                    def chunk_stats(n, c, h, size):
                        dve.wait_ge(s_relu, 2 * n + h + 3)
                        return nc.vector.bn_stats(stats4[:, h, bass.ds(c, 1), :].rearrange("p c s -> p (c s)"),
                                                  hT3[:, h, bass.ds(c * CH, size)])
                    n0 = l * NCH
                    combine(n0, 0, 0, n0 + 1)
                    combine(n0, 0, 1, n0 + 1)
                    chunk_stats(n0, 0, 0, CH)

                    def chunk(c, split):
                        combine(n0 + c, c, 0, n0 + c + 2)
                        chunk_stats(n0 + c - 1, c - 1, 1, CH)
                        if split:
                            split_weights(l + 1)
                        combine(n0 + c, c, 1, n0 + c + 2)
                        chunk_stats(n0 + c, c, 0, CH)
                    with dve.Fori(1, LAST - 1) as c:
                        chunk(c, False)
                    chunk(LAST - 1, more)
                    combine(n0 + LAST, LAST, 0, n0 + NCH)
                    chunk_stats(n0 + LAST - 1, LAST - 1, 1, CH)
                    combine(n0 + LAST, LAST, 1, n0 + NCH)
                    count = [0]

                    def chain(ins):
                        count[0] += 1
                        ins.then_inc(s_chain, 1)
                        dve.wait_ge(s_chain, l * CHAIN + base + count[0])
                    chunk_stats(n0 + LAST, LAST, 0, TAIL)
                    chain(chunk_stats(n0 + LAST, LAST, 1, TAIL))
                    nc.vector.memset(bn_shift, 0.0)
                    for f in range(HALVES):
                        last = nc.vector.bn_aggr(bn_mv[:, f], stats4[:, f].rearrange("p c s -> p (c s)"))
                    chain(last)
                    nc.vector.tensor_scalar(bn_v, bn_mv[:, :, 1], EPS, None, ALU.add).then_inc(s_bnvar, 1)
                    dve.wait_ge(s_bnvar, l + 1)
                    dve.wait_ge(s_bnroot, l + 1)
                    cols = bass.ds(l * HALVES, HALVES)
                    newton(bn_v, bn_r, bn_t, aff[:, 1, cols], bn_scale, chain)
                    chain(nc.vector.scalar_tensor_tensor(bn_t, bn_mv[:, :, 0], -1.0, bn_scale, ALU.mult, ALU.mult))
                    chain(nc.vector.tensor_tensor(bn_shift, bn_t, aff[:, 2, cols], ALU.add))
                    assert count[0] == CHAIN, count
                    dve.sem_inc(s_affine, 1)

                layer(0, True, True)
                with dve.Fori(1, L - 1) as l:
                    layer(l, False, True)
                layer(L - 1, False, False)
                for g in range(NCH):
                    cols = slice(g * CH, g * CH + width(g))
                    nc.vector.tensor_scalar(hT3[:, 1, cols], hT3[:, 1, cols], bn_scale[:, 1:2], bn_shift[:, 1:2], ALU.mult,
                                            ALU.add).then_inc(s_final[1], 1)
                for i in range(BLOCKS):
                    n = nodes(i)
                    if i % BQ == 0:
                        dve.wait_ge(s_xr[i // BQ], 32 if i // BQ == NBQ - 1 else 16)
                    dve.wait_ge(s_back, i + 1)
                    nc.vector.tensor_tensor(out_tiles[0:n, i], banks[2 + i % TB][0:n, 0:D], x_again[0:n, i], ALU.add).then_inc(s_res, 1)

            @block.scalar
            def _(act):
                act.wait_ge(s_var, 1)
                nc.scalar.activation(ln_r, ln_v, ACT.Sqrt).then_inc(s_root, 1)

                def split_weights(l):
                    act.wait_ge(s_w, 16 * l + 16)
                    nc.scalar.mul(weights[:, 0], staged, WMUL).then_inc(s_whi, 1)
                act.wait_ge(s_ln, 1)
                for i in range(BLOCKS + TB):
                    if i < BLOCKS and i % 2 == 0:
                        n = nodes(i)
                        nc.scalar.activation(x_tiles[0:n, i], x_tiles[0:n, i], ACT.Identity, bias=ln_b[0:n, i:i + 1],
                                             scale=ln_r[0:n, i:i + 1]).then_inc(s_hn[0], 1)
                    if i >= TB:
                        j = i - TB
                        n, c = nodes(j), j // CB
                        act.wait_ge(s_h0T, j + 1)
                        nc.scalar.activation(parts(0, c, (j % CB) * P, n), both_halves(j, n), ACT.Relu).then_inc(s_h0hi, 1)
                    if i == BLOCKS // 2:
                        split_weights(0)
                act.wait_ge(s_lnz, BLOCKS + 1)
                act.sem_inc(s_relu, 2)

                def high_features(l, q):
                    g, at, n = PIECES[q]
                    act.wait_ge(s_linear, (l - 1) * NPC + q + 1)
                    nc.scalar.activation(parts(0, g, at, n), linear[g % 2][:, :, at:at + n], ACT.Relu).then_inc(s_hhi, 1)

                def layer(l, first, more):
                    if not first:
                        high_features(l, 0)
                        high_features(l, 1)
                    for i in range(BLOCKS):
                        n, g = nodes(i), i // CB
                        act.wait_ge(s_msg, l * BLOCKS + i + 1)
                        nc.scalar.activation(hs4[0:n, i, 0], banks[4 + i % MB][0:n, 0:D], ACT.Copy,
                                             scale=dcol[0:n, i:i + 1]).then_inc(s_hi, 1)
                        if not first and i % CB == 0 and g + 2 < NPC:
                            high_features(l, g + 2)
                        if i == CB - 1:
                            act.wait_ge(s_eww, l + 1)
                            nc.scalar.mul(hs4[EWR, BLOCKS - 1, 0], banks[7][EWR, 0:D], ZSCALE).then_inc(s_ewhi, 1)

                    def relu(n, c, h):
                        act.wait_ge(s_comb, 2 * n + h + 1)
                        nc.scalar.activation(hT3[:, h, bass.ds(c * CH, width(c))], summed[:, h, 0:width(c)], ACT.Relu,
                                             bias=bias_now[:, h:h + 1]).then_inc(s_relu, 1)
                    with act.Fori(0, LAST - 1) as c:
                        for h in range(HALVES):
                            relu(l * NCH + c, c, h)
                    relu(l * NCH + LAST - 1, LAST - 1, 0)
                    if more:
                        act.wait_ge(s_own, l * NCH + NCH)
                        split_weights(l + 1)
                    relu(l * NCH + LAST - 1, LAST - 1, 1)
                    for h in range(HALVES):
                        relu(l * NCH + LAST, LAST, h)

                def root(l):
                    act.wait_ge(s_bnvar, l + 1)
                    nc.scalar.activation(bn_r, bn_v, ACT.Sqrt).then_inc(s_bnroot, 1)
                    act.wait_ge(s_affine, l + 1)

                layer(0, True, True)
                root(0)
                with act.Fori(1, L - 1) as l:
                    layer(l, False, True)
                    root(l)
                layer(L - 1, False, False)
                root(L - 1)
                for g in range(NCH):
                    cols = slice(g * CH, g * CH + width(g))
                    nc.scalar.activation(hT3[:, 0, cols], hT3[:, 0, cols], ACT.Identity, bias=bn_shift[:, 0:1],
                                         scale=bn_scale[:, 0:1]).then_inc(s_final[0], 1)

            @block.tensor
            def _(pe):
                for i in range(BLOCKS):
                    n = nodes(i)
                    pe.wait_ge(s_hn[i % 2], i // 2 + 1)
                    if i >= TB:
                        pe.wait_ge(s_lnz, i - TB + 1)
                    for f in range(HALVES):
                        last = nc.tensor.transpose(banks[2 + i % TB][:, f * P:f * P + n], x_tiles[0:n, i, f * P:(f + 1) * P],
                                                   ident[0:n, 0:n])
                    last.then_inc(s_h0T, 1)

                def edge_weights(l):
                    pe.wait_ge(s_ewnow, l + 1)
                    for f in range(HALVES):
                        last = nc.tensor.matmul(banks[7][EWR, 0:D], ew_now[:, f, :], staged[:, 2 + f, :],
                                                start=(f == 0), stop=(f == HALVES - 1))
                    last.then_inc(s_eww, 1)

                def message(l, i):
                    n = nodes(i)
                    if block_piece(i) is not None:
                        pe.wait_ge(s_norm, l * NPC + block_piece(i) + 1)
                    for f in range(HALVES):
                        for s, ws in PASSES:
                            last = nc.tensor.matmul(banks[4 + i % MB][0:n, 0:D], part(f, s, i // CB, (i % CB) * P, n),
                                                    weights[:, ws, 2 + f, :], start=(f == 0 and s + ws == 0),
                                                    stop=(f == HALVES - 1 and s == 1))
                    last.then_inc(s_msg, 1)

                def layer(l):
                    edge_weights(l)
                    for i in range(MB):
                        message(l, i)
                    for i in range(BLOCKS):
                        pe.wait_ge(s_parts, l * BLOCKS + i + 1)
                        if i == BLOCKS - 1:
                            pe.wait_ge(s_ewparts, l + 1)
                        for h in range(2):
                            if i == 0:
                                pe.wait_ge(s_scaled[h], l * NCH + 1)
                            for s in range(2):
                                last = nc.tensor.matmul(banks[h][:, 0:CH], hs4[:, i, s, h * P:(h + 1) * P],
                                                        countsT[:, i * NP:i * NP + CH],
                                                        start=(i == 0 and s == 0), stop=(i == BLOCKS - 1 and s == 1))
                            if i == BLOCKS - 1:
                                last.then_inc(s_sum[h], 1)
                            if h == 0 and i + MB < BLOCKS:
                                message(l, i + MB)

                    def sums(n, c, h):
                        w = width(c)
                        pe.wait_ge(s_scaled[h], n + 1)
                        for i in range(BLOCKS):
                            for s in range(2):
                                last = nc.tensor.matmul(banks[h][:, 0:w], hs4[:, i, s, h * P:(h + 1) * P],
                                                        countsT[:, bass.ds(c * CH + i * NP, w)],
                                                        start=(i == 0 and s == 0), stop=(i == BLOCKS - 1 and s == 1))
                        last.then_inc(s_sum[h], 1)

                    def own(c):
                        w = width(c)
                        for h in range(2):
                            to = banks[6][:, h * LO:h * LO + w] if w < CH else banks[2 + h][:, 0:w]
                            for f in range(HALVES):
                                for s, ws in PASSES:
                                    last = nc.tensor.matmul(to, weights[:, ws, f, h * P:(h + 1) * P], part(f, s, c, 0, w),
                                                            start=(f == 0 and s + ws == 0), stop=(f == HALVES - 1 and s == 1))
                        last.then_inc(s_own, 1)

                    n0 = l * NCH
                    own(0)
                    own(LAST)
                    with pe.Fori(1, LAST) as c:
                        sums(n0 + c, c, 0)
                        pe.wait_ge(s_comb, 2 * (n0 + c))
                        own(c)
                        sums(n0 + c, c, 1)
                    sums(n0 + LAST, LAST, 0)
                    sums(n0 + LAST, LAST, 1)

                with pe.Fori(0, L) as l:
                    layer(l)
                for i in range(BLOCKS):
                    n = nodes(i)
                    if i % CB == 0:
                        for f in range(HALVES):
                            pe.wait_ge(s_final[f], i // CB + 1)
                    if i >= TB:
                        pe.wait_ge(s_res, i - TB + 1)
                    for f in range(HALVES):
                        last = nc.tensor.transpose(banks[2 + i % TB][0:n, f * P:(f + 1) * P], hT3[:, f, i * P:i * P + n],
                                                   ident[:, :])
                    last.then_inc(s_back, 1)


_INS = ["x", "src", "dst", "edge_attr_4", "L0_gnn_mlp_w", "L0_gnn_mlp_b", "L0_gnn_ew1", "L0_gnn_ew2", "L0_gnn_bn_g", "L0_gnn_bn_b"]


def kernel(**inputs):
    import numpy as _np
    import concourse.bacc as _bacc
    from concourse import mybir as _mybir
    from concourse.bass_utils import run_bass_kernel_spmd as _run

    nc = _bacc.Bacc("TRN2", target_bir_lowering=False, num_devices=1, dynamic_dma_scratch_size=1024)
    arrays, args = {}, []
    for name in _INS:
        a = _np.ascontiguousarray(inputs[name])
        arrays[f"in_{name}"] = a
        args.append(nc.dram_tensor(f"in_{name}", a.shape, _mybir.dt.from_np(a.dtype), kind="ExternalInput").ap())
    shape = inputs["x"].shape
    args.append(nc.dram_tensor("out_0", shape, _mybir.dt.float32, kind="ExternalOutput").ap())
    gnn_program(nc, *args)
    r = _run(nc, [arrays], core_ids=[0])
    return r.results[0]["out_0"]
```
